# Optimizing a Trainium2 kernel written in Bass

```python
import numpy as np
import jax
import jax.numpy as jnp

def _softmax(x, axis=-1):
    return jax.nn.softmax(x, axis=axis)

def _gelu(x):
    return jax.nn.gelu(x, approximate=True)

def _silu(x):
    return jax.nn.silu(x)

def _sigmoid(x):
    return jax.nn.sigmoid(x)

def _layernorm(x, axis=-1, eps=1e-05):
    m = jnp.mean(x, axis=axis, keepdims=True)
    v = jnp.var(x, axis=axis, keepdims=True)
    return (x - m) / jnp.sqrt(v + eps)

def _scatter_add(tgt, idx, src, axis=0):
    return tgt.at[idx].add(src)

def _segment_sum(src, seg, n):
    return jax.ops.segment_sum(src, seg, n)
kernel_name = 'mk_gnn_resnorm_d1_gnn_r32_dfb0d1'

def setup_inputs(seed: int=0):
    np.random.seed(seed)
    _w = jnp.asarray

    def _rec_inputs():
        import jax
        import jax.numpy as jnp
        _gk = jax.random.key(seed)
        x = 0.0001712 + 1 * jax.random.normal(jax.random.fold_in(_gk, 1), (3125, 16), jnp.float32)
        src = jax.random.randint(jax.random.fold_in(_gk, 2), (100000,), 0, 3125, jnp.int32)
        dst = jax.random.randint(jax.random.fold_in(_gk, 3), (100000,), 0, 3125, jnp.int32)
        _o = jnp.argsort(dst, stable=True)
        src = src[_o]
        dst = dst[_o]
        edge_attr_6 = jax.random.uniform(jax.random.fold_in(_gk, 11), (100000, 6), jnp.float32, 0.0, 1)
        return (x, src, dst, edge_attr_6)
    x, src, dst, edge_attr_6 = _rec_inputs()

    def _L0_gnn_setup():
        import jax, jax.numpy as jnp
        import numpy as np
        LATENT = 16
        KDIM = 128
        EDIM = 6
        DEPTH = 4
        N_NODES = 50000
        N_EDGES = 25000

        def _kernel_net(edge_attr, kW1, kb1, kW2, kb2, kW3, kb3):
            h = jax.nn.gelu(edge_attr @ kW1 + kb1)
            h = jax.nn.gelu(h @ kW2 + kb2)
            return h @ kW3 + kb3
        key = jax.random.key(seed)
        ks = jax.random.split(key, 12)
        inp = {'nodes': jax.random.normal(ks[0], (N_NODES, LATENT), dtype=jnp.float32), 'edge_index': jax.random.randint(ks[1], (2, N_EDGES), 0, N_NODES, dtype=jnp.int64), 'edge_attr': jax.random.uniform(ks[2], (N_EDGES, EDIM), dtype=jnp.float32), 'kW1': jax.random.normal(ks[3], (EDIM, KDIM), dtype=jnp.float32) / np.sqrt(EDIM), 'kb1': jnp.zeros((KDIM,), dtype=jnp.float32), 'kW2': jax.random.normal(ks[4], (KDIM, KDIM), dtype=jnp.float32) / np.sqrt(KDIM), 'kb2': jnp.zeros((KDIM,), dtype=jnp.float32), 'kW3': jax.random.normal(ks[5], (KDIM, LATENT * LATENT), dtype=jnp.float32) / np.sqrt(KDIM), 'kb3': jnp.zeros((LATENT * LATENT,), dtype=jnp.float32), 'root_W': jax.random.normal(ks[6], (DEPTH, LATENT, LATENT), dtype=jnp.float32) / np.sqrt(LATENT), 'root_b': jnp.zeros((DEPTH, LATENT), dtype=jnp.float32)}
        return inp
    _L0_gnn_all = _L0_gnn_setup()
    _L0_gnn_in = {k: v for k, v in _L0_gnn_all.items() if k in ('kW1', 'kb1', 'kW2', 'kb2', 'kW3', 'kb3', 'root_W', 'root_b')}
    del _L0_gnn_all
    return {'x': x, 'src': src, 'dst': dst, 'edge_attr_6': edge_attr_6, 'L0_gnn_kW1': _L0_gnn_in['kW1'], 'L0_gnn_kb1': _L0_gnn_in['kb1'], 'L0_gnn_kW2': _L0_gnn_in['kW2'], 'L0_gnn_kb2': _L0_gnn_in['kb2'], 'L0_gnn_kW3': _L0_gnn_in['kW3'], 'L0_gnn_kb3': _L0_gnn_in['kb3'], 'L0_gnn_root_W': _L0_gnn_in['root_W'], 'L0_gnn_root_b': _L0_gnn_in['root_b']}

def reference(x, src, dst, edge_attr_6, L0_gnn_kW1, L0_gnn_kb1, L0_gnn_kW2, L0_gnn_kb2, L0_gnn_kW3, L0_gnn_kb3, L0_gnn_root_W, L0_gnn_root_b):
    import jax
    import jax.numpy as jnp

    def _L0_gnn_ref(nodes, edge_attr, kW1, kb1, kW2, kb2, kW3, kb3, root_W, root_b, edge_index):
        import jax, jax.numpy as jnp
        import numpy as np
        LATENT = 16
        KDIM = 128
        EDIM = 6
        DEPTH = 4
        N_NODES = 50000
        N_EDGES = 25000

        def _kernel_net(edge_attr, kW1, kb1, kW2, kb2, kW3, kb3):
            h = jax.nn.gelu(edge_attr @ kW1 + kb1)
            h = jax.nn.gelu(h @ kW2 + kb2)
            return h @ kW3 + kb3
        src, dst = (edge_index[0], edge_index[1])
        n = nodes.shape[0]
        w = _kernel_net(edge_attr, kW1, kb1, kW2, kb2, kW3, kb3).reshape(-1, LATENT, LATENT)
        deg = jax.ops.segment_sum(jnp.ones((src.shape[0],), nodes.dtype), dst, num_segments=n)
        inv_deg = jnp.where(deg > 0, 1.0 / jnp.maximum(deg, 1.0), 0.0)[:, None]
        for i in range(DEPTH):
            msg = jnp.einsum('ei,eio->eo', nodes[src], w)
            agg = jax.ops.segment_sum(msg, dst, num_segments=n)
            agg = agg * inv_deg
            nodes = jax.nn.gelu(agg + nodes @ root_W[i] + root_b[i])
        return nodes
    edge_index = jnp.stack([src, dst])
    x = _layernorm(x + _L0_gnn_ref(x, edge_attr_6, L0_gnn_kW1, L0_gnn_kb1, L0_gnn_kW2, L0_gnn_kb2, L0_gnn_kW3, L0_gnn_kb3, L0_gnn_root_W, L0_gnn_root_b, edge_index), axis=-1)
    return x

_drawn_inputs = setup_inputs


def setup_inputs(seed=0):
    import zlib

    import numpy as np

    out = dict(_drawn_inputs(seed))
    spreads = {'L0_gnn_kb1': (0.0, 0.443),
     'L0_gnn_kb2': (0.0, 0.1),
     'L0_gnn_kb3': (0.0, 0.1),
     'L0_gnn_root_b': (0.0, 0.1)}
    factors = {'edge_attr_6': 3.866}
    for name, (base, spread) in spreads.items():
        noise = np.random.default_rng([zlib.crc32(name.encode()), seed]).standard_normal(out[name].shape)
        drawn = base * np.exp(spread * noise) if base else spread * noise
        out[name] = jnp.asarray(drawn.astype(out[name].dtype))
    for name, factor in factors.items():
        out[name] = (out[name] * factor).astype(out[name].dtype)
    return out
```

```python
import concourse.bass as bass
from concourse import mybir
from contextlib import ExitStack

F32 = mybir.dt.float32
BF16 = mybir.dt.bfloat16
I32 = mybir.dt.int32
U32 = mybir.dt.uint32
ALU = mybir.AluOpType
ACT = mybir.ActivationFunctionType
AX = mybir.AxisListType

P = 128
TG = 16
SL = 8
NOWHERE = 1.0e6
EPS = 1e-5


def layout(n_nodes, n_edges, lat):
    lo = -(-n_nodes // P)
    hi = n_nodes // lo
    assert hi * lo == n_nodes and (lat + 1) * lo <= 512
    tiles = -(-n_edges // (P * TG)) * TG
    return dict(LO=lo, HI=hi, NT=tiles, NG=tiles // TG, RB=-(-tiles // P))


def constants(n_nodes, n_edges, lat):
    d = layout(n_nodes, n_edges, lat)
    at, cols = 0, {}
    for name, n in (("ident", P), ("slot_tile", TG), ("slot", 1), ("slots", SL),
                    ("first_of_hi", d["HI"]), ("his", d["HI"]), ("los", d["LO"])):
        cols[name] = (at, at + n)
        at += n
    return cols, at


def at_least(eng, sem, value):
    if not isinstance(value, int) or value > 0:
        eng.wait_ge(sem, value)


def gnn_kernel(nc, x, src, dst, edge_attr, kW1, kb1, kW2, kb2, kW3, kb3, root_W, root_b, consts, out):
    N, LAT = x.shape
    E, ED = edge_attr.shape
    K = kW2.shape[0]
    DEPTH = root_W.shape[0]
    d = layout(N, E, LAT)
    LO, HI, NT, NG, RB = d["LO"], d["HI"], d["NT"], d["NG"], d["RB"]
    cols, ncols = constants(N, E, LAT)
    NW = -(-N // SL)
    FULL, REST = E // P, E % P
    NL = LO * LAT
    NLD = NL + LO
    PER = TG * LAT
    CB = 8 * LAT
    NCB = -(-NL // CB)
    PAIRS = (NG - 3) // 2
    assert NG % 2 == 1 and NG >= 5 and K == P and TG * SL == P

    nodes_dram = nc.dram_tensor("nodes_scratch", (N, LAT), F32).ap()
    h2_dram = nc.dram_tensor("h2_scratch", (NG * P, TG * K), F32).ap()

    ctx = ExitStack()
    with ctx:
        def sb(name, shape, dt=F32):
            return ctx.enter_context(nc.sbuf_tensor(name, shape, dt))

        def sem(name):
            return ctx.enter_context(nc.semaphore(name))

        cst = sb("cst", [P, ncols])
        ident = cst[:, cols["ident"][0]:cols["ident"][1]]
        slot_tile = cst[:, cols["slot_tile"][0]:cols["slot_tile"][1]]
        slot = cst[:, cols["slot"][0]:cols["slot"][1]]
        slots = cst[:, cols["slots"][0]:cols["slots"][1]]
        first_of_hi = cst[:, cols["first_of_hi"][0]:cols["first_of_hi"][1]]
        his = cst[:, cols["his"][0]:cols["his"][1]]
        los = cst[:, cols["los"][0]:cols["los"][1]]
        ones = sb("ones", [P, P])
        w1 = sb("w1", [P, K])
        w2 = sb("w2", [K, K])
        w3 = sb("w3", [K, LAT * LAT])
        b3 = sb("b3", [LAT, LAT])
        b1 = sb("b1", [K, 1])
        b2 = sb("b2", [K, 1])
        root = sb("root", [P, DEPTH, P])
        rb = sb("rb", [P, DEPTH, LAT])
        rows_i = sb("rows_i", [P, 2, RB, P], I32)
        rows_f = sb("rows_f", [P, 2, RB, P])
        real = sb("real", [P, RB, P])
        least = sb("least", [P, RB])
        most = sb("most", [P, RB])
        wide = sb("wide", [P, RB])
        wide_any = sb("wide_any", [P, 1])
        narrow = sb("narrow", [P, 1])
        flag = sb("flag", [P, 1], I32)
        diag = sb("diag", [P, RB, P])
        src_e = sb("src_e", [P, NT], U32)
        dst_e = sb("dst_e", [P, NT])
        base0 = sb("base0", [P, NT])
        base = sb("base", [P, NT])
        rel = sb("rel", [P, NT])
        picked = sb("picked", [P, NG, TG])
        node = sb("node", [P, NG])
        below = sb("below", [P, NG, HI])
        node_hi = sb("node_hi", [P, NG])
        node_lo = sb("node_lo", [P, NG])
        attr = [sb(f"attr{b}", [P, TG, 32]) for b in range(2)]
        attrT = sb("attrT", [P, 4 * P])
        h1 = [sb(f"h1_{b}", [K, 4 * P]) for b in range(2)]
        h2T = [sb(f"h2T_{b}", [K, 4 * P]) for b in range(2)]
        h2 = [sb(f"h2_{b}", [P, TG, K]) for b in range(2)]
        ix = [sb(f"ix{b}", [P, TG], U32) for b in range(2)]
        xe = [sb(f"xe{b}", [P, TG, LAT]) for b in range(2)]
        in_slot = [sb(f"in_slot{b}", [P, TG, SL]) for b in range(2)]
        xs = [sb(f"xs{b}", [P, TG, SL, LAT]) for b in range(2)]
        g_sb = [sb(f"g_sb{b}", [K, TG, SL, LAT]) for b in range(2)]
        xsum = sb("xsum", [LAT, P])
        part = [sb(f"part{s}", [P, LAT + 1], BF16) for s in range(3)]
        left = [sb(f"left{s}", [P, LAT]) for s in range(2)]
        hot_hi = [sb(f"hot_hi{b}", [P, HI], BF16) for b in range(2)]
        hot_lo = sb("hot_lo", [P, LO], BF16)
        spread = [sb(f"spread{b}", [P, 3, NLD], BF16) for b in range(2)]
        x0 = sb("x0", [P, LO, LAT])
        xn = sb("xn", [P, LO, LAT])
        agg = sb("agg", [P, NLD])
        inv = sb("inv", [P, LO])
        xT = sb("xT", [P, NCB, HI])
        root_l = sb("root_l", [P, P])
        rb_l = sb("rb_l", [P, LAT])
        pre = sb("pre", [P, LO, LAT])
        mean = sb("mean", [P, LO])
        var = sb("var", [P, LO])
        sq = sb("sq", [P, LO, LAT])

        bank = [ctx.enter_context(nc.psum_tensor(f"bank{i}", [P, 512], F32)) for i in range(8)]
        ps_g = bank[0:2]
        ps_agg = bank[2]
        ps_slot = bank[3][:, 0:LAT]
        ps_deg = bank[3][:, LAT:LAT + 1]
        ps_xsum = bank[4][0:LAT, 0:P]
        ps_attr, ps_1, ps_2, ps_t = bank[4:8]

        s_chain = sem("s_chain")
        s_load = sem("s_load")
        s_fill = sem("s_fill")
        s_rows = sem("s_rows")
        s_mm = sem("s_mm")
        s_copied = sem("s_copied")
        first_sem = [sem("attr_loaded0"), sem("attr_loaded1")]
        attr_loaded = first_sem
        attr_turned = sem("attr_turned")
        attrT_ready = sem("attrT_ready")
        mm1_done = sem("mm1_done")
        h1_ready = sem("h1_ready")
        mm2_done = sem("mm2_done")
        h2T_ready = sem("h2T_ready")
        h2_turned = sem("h2_turned")
        h2_ready = sem("h2_ready")
        h2_stored = [sem("h2_stored0"), sem("h2_stored1")]
        h2_loaded = [sem("h2_loaded0"), sem("h2_loaded1")]
        ix_ready = sem("ix_ready")
        gathers_begun = sem("gathers_begun")
        gathered = [sem("gathered0"), sem("gathered1")]
        in_slot_ready = sem("in_slot_ready")
        xs_ready = sem("xs_ready")
        g_done = sem("g_done")
        g_copied = sem("g_copied")
        xsum_done = sem("xsum_done")
        xsum_copied = sem("xsum_copied")
        slot_done = sem("slot_done")
        hot_ready = sem("hot_ready")
        split_step = sem("split_step")
        slot_read = sem("slot_read")
        spread_ready = sem("spread_ready")
        scattered = sem("scattered")
        agg_ready = sem("agg_ready")
        every = [s_chain, s_load, s_fill, s_rows, s_mm, s_copied, *attr_loaded, attr_turned, attrT_ready,
                 mm1_done, h1_ready, mm2_done, h2T_ready, h2_turned, h2_ready, *h2_stored, *h2_loaded,
                 ix_ready, gathers_begun, *gathered, in_slot_ready, xs_ready, g_done, g_copied, xsum_done, xsum_copied,
                 slot_done, hot_ready, split_step, slot_read, spread_ready, scattered, agg_ready]

        def clear_counts():
            with nc.Block() as block:
                @block.gpsimd
                def _(pool):
                    pool.dma_reset()
                    for s in every:
                        pool.sem_clear(s)

        def setup():
            block = ctx2.enter_context(nc.Block())

            @block.sync
            def _(sp):
                sp.dma_start(cst[:, :], consts).then_inc(s_load, 16)
                sp.dma_start(w2[:, :], kW2).then_inc(s_load, 16)
                sp.dma_start(w3[:, :], kW3).then_inc(s_load, 16)
                sp.dma_start(b3[:, :], kb3.rearrange("(i o) -> i o", i=LAT)).then_inc(s_load, 16)
                sp.dma_start(b1[:, :], kb1.rearrange("(k a) -> k a", a=1)).then_inc(s_load, 16)
                sp.dma_start(b2[:, :], kb2.rearrange("(k a) -> k a", a=1)).then_inc(s_load, 16)
                for j in range(4):
                    sp.dma_start(w1[32 * j:32 * j + ED, :], kW1).then_inc(s_load, 16)
                x_rows = x.rearrange("(h l) f -> h (l f)", l=LO)
                sp.dma_start(x0[0:HI, :, :].rearrange("p l f -> p (l f)"), x_rows).then_inc(s_load, 16)
                sp.dma_start(xn[0:HI, :, :].rearrange("p l f -> p (l f)"), x_rows).then_inc(s_load, 16)
                sp.dma_start(rb[:, :, :], root_b.rearrange("(a l) o -> a l o", a=1)
                             .to_broadcast([P, DEPTH, LAT])).then_inc(s_load, 16)
                sp.wait_ge(s_fill, 1)
                for q in range(8):
                    sp.dma_start(root[LAT * q:LAT * (q + 1), :, LAT * q:LAT * (q + 1)],
                                 root_W.rearrange("l i o -> i l o")).then_inc(s_load, 16)
                sp.wait_ge(s_fill, 3)
                for w, a in enumerate((src, dst)):
                    whole = FULL // P
                    if whole:
                        sp.dma_start(rows_i[:, w, 0:whole, :],
                                     a[0:whole * P * P].rearrange("(g r e) -> r g e", r=P, e=P)).then_inc(s_rows, 16)
                    more = FULL - whole * P
                    if more:
                        sp.dma_start(rows_i[0:more, w, whole, :],
                                     a[whole * P * P:FULL * P].rearrange("(r e) -> r e", e=P)).then_inc(s_rows, 16)
                    if REST:
                        sp.dma_start(rows_i[more:more + 1, w, whole, 0:REST],
                                     a[FULL * P:E].rearrange("(r e) -> r e", r=1)).then_inc(s_rows, 16)
                sp.wait_ge(s_load, 16 * 21)

            n_rows = 16 * 2 * (bool(FULL // P) + bool(FULL % P) + bool(REST))

            @block.gpsimd
            def _(pool):
                pool.memset(root[:, :, :], 0.0).then_inc(s_fill, 1)
                pool.memset(rows_i[:, 0, :, :], 0).then_inc(s_fill, 1)
                pool.memset(rows_i[:, 1, :, :], int(NOWHERE)).then_inc(s_fill, 1)
                pool.memset(ones[:, :], 1.0).then_inc(s_fill, 1)
                for b in range(2):
                    pool.memset(attr[b][:, :, :], 0.0)
                pool.memset(agg[:, :], 0.0)

            @block.vector
            def _(dve):
                done = [0]

                def link(ins):
                    done[0] += 1
                    ins.then_inc(s_chain, 1)
                    dve.wait_ge(s_chain, done[0])

                dve.wait_ge(s_load, 16 * 21)
                dve.wait_ge(s_rows, n_rows)
                link(nc.vector.tensor_copy(rows_f[:, :, :, :], rows_i[:, :, :, :]))
                link(nc.vector.tensor_reduce(least[:, :], rows_f[:, 1, :, :], AX.X, ALU.min))
                link(nc.vector.scalar_tensor_tensor(real[:, :, :], rows_f[:, 1, :, :], NOWHERE / 2,
                                                    rows_f[:, 1, :, :], ALU.is_lt, ALU.mult))
                link(nc.vector.tensor_reduce(most[:, :], real[:, :, :], AX.X, ALU.max))
                link(nc.vector.tensor_tensor(wide[:, :], most[:, :], least[:, :], ALU.subtract))
                link(nc.vector.tensor_scalar(wide[:, :], wide[:, :], float(SL - 1), None, ALU.is_gt))
                link(nc.vector.tensor_reduce(wide_any[:, :], wide[:, :], AX.X, ALU.add))
                for r in range(RB):
                    link(nc.vector.tensor_scalar(diag[:, r, :], ident, least[:, r:r + 1], None, ALU.mult))
                for r in range(RB):
                    n = min(P, NT - r * P)
                    at = slice(r * P, r * P + n)
                    dve.wait_ge(s_mm, r + 1)
                    nc.vector.tensor_copy(base0[:, at], bank[r % 2][:, 0:n])
                    nc.vector.tensor_copy(src_e[:, at], bank[r % 2][:, P:P + n])
                    nc.vector.tensor_copy(dst_e[:, at], bank[r % 2][:, 2 * P:2 * P + n]).then_inc(s_copied, 1)
                dve.wait_ge(s_mm, RB + 1)
                link(nc.vector.tensor_copy(flag[:, :], bank[2][:, 0:1]))
                link(nc.vector.tensor_scalar(narrow[:, :], bank[2][:, 0:1], 0.5, None, ALU.is_lt))
                nc.vector.tensor_scalar(base0[:, :], base0[:, :], narrow[:, :], None, ALU.mult)

            @block.tensor
            def _(pe):
                pe.wait_ge(s_fill, 4)
                pe.wait_ge(s_chain, 7 + RB)
                for r in range(RB):
                    if r >= 2:
                        pe.wait_ge(s_copied, r - 1)
                    nc.tensor.matmul(bank[r % 2][:, 0:P], ones[:, :], diag[:, r, :], start=True, stop=True)
                    nc.tensor.transpose(bank[r % 2][:, P:2 * P], rows_f[:, 0, r, :], ident)
                    nc.tensor.transpose(bank[r % 2][:, 2 * P:3 * P], rows_f[:, 1, r, :], ident).then_inc(s_mm, 1)
                nc.tensor.matmul(bank[2][:, 0:1], ones[:, :], wide_any[:, :], start=True, stop=True).then_inc(s_mm, 1)

        def windows(new_base):
            with nc.Block() as block:
                @block.vector
                def _(dve):
                    done = [0]

                    def link(ins):
                        done[0] += 1
                        ins.then_inc(s_chain, 1)
                        dve.wait_ge(s_chain, done[0])

                    if new_base == "first":
                        link(nc.vector.tensor_copy(base[:, :], base0[:, :]))
                    if new_base == "next":
                        link(nc.vector.tensor_scalar(base[:, :], base[:, :], float(SL), None, ALU.add))
                    link(nc.vector.tensor_tensor(rel[:, :], dst_e[:, :], base[:, :], ALU.subtract))
                    link(nc.vector.tensor_tensor(picked[:, :, :], base[:, :].rearrange("p (g t) -> p g t", t=TG),
                                                 slot_tile.unsqueeze(1).to_broadcast([P, NG, TG]), ALU.mult))
                    link(nc.vector.tensor_reduce(node[:, :], picked[:, :, :], AX.X, ALU.add))
                    link(nc.vector.tensor_scalar(node[:, :], node[:, :], slot, None, ALU.add))
                    link(nc.vector.tensor_tensor(below[:, :, :], node[:, :].unsqueeze(2).to_broadcast([P, NG, HI]),
                                                 first_of_hi.unsqueeze(1).to_broadcast([P, NG, HI]), ALU.is_ge))
                    link(nc.vector.tensor_reduce(node_hi[:, :], below[:, :, :], AX.X, ALU.add))
                    link(nc.vector.tensor_scalar(node_hi[:, :], node_hi[:, :], -1.0, None, ALU.add))
                    link(nc.vector.scalar_tensor_tensor(node_lo[:, :], node_hi[:, :], -float(LO), node[:, :],
                                                        ALU.mult, ALU.add))
            clear_counts()

        def edge_pass(table, with_mlp):
            block_ctx = nc.Block()
            block = block_ctx.__enter__()

            def over_groups(eng, step):
                step(0, 0, 0)
                step(1, 1, 0)
                with eng.Fori(1, 1 + PAIRS) as h:
                    step(h * 2, 0, h)
                    step(h * 2 + 1, 1, h)
                step(NG - 1, 0, (NG - 1) // 2)

            @block.sync
            def _(sp):
                def store(g, b):
                    sp.wait_ge(h2_ready, 4 * (g + 1))
                    sp.dma_start(h2_dram[bass.ds(g * P, P), :], h2[b][:, :, :].rearrange("p t k -> p (t k)"))\
                      .then_inc(h2_stored[b], 16)

                def step(g, b, half):
                    if not with_mlp:
                        at_least(sp, g_done, 4 * (g - 1))
                        sp.dma_start(h2[b][:, :, :].rearrange("p t k -> p (t k)"),
                                     h2_dram[bass.ds(g * P, P), :]).then_inc(h2_loaded[b], 16)
                        return
                    at_least(sp, attr_turned, g - 1)
                    if isinstance(g, int) and g == NG - 1:
                        t = FULL - g * TG
                        if t:
                            sp.dma_start(attr[b][:, 0:t, 0:ED], edge_attr[g * TG * P:FULL * P, :]
                                         .rearrange("(t e) f -> e t f", e=P)).then_inc(attr_loaded[b], 16)
                        if REST:
                            sp.dma_start(attr[b][0:REST, t, 0:ED], edge_attr[FULL * P:E, :]).then_inc(attr_loaded[b], 16)
                    else:
                        sp.dma_start(attr[b][:, :, 0:ED], edge_attr[bass.ds(g * (TG * P), TG * P), :]
                                     .rearrange("(t e) f -> e t f", e=P)).then_inc(attr_loaded[b], 16)
                    if not isinstance(g, int) or g >= 1:
                        store(g - 1, 1 - b)

                over_groups(sp, step)
                if with_mlp:
                    store(NG - 1, 0)
                    sp.wait_ge(h2_stored[0], 16 * (NG - NG // 2))
                    sp.wait_ge(h2_stored[1], 16 * (NG // 2))

            last_loads = 16 * (bool(FULL - (NG - 1) * TG) + bool(REST))

            @block.gpsimd
            def _(pool):
                def step(g, b, half):
                    at_least(pool, gathered[b], half * (16 * TG))
                    nc.gpsimd.tensor_copy(ix[b][:, :], src_e[:, bass.ds(g * TG, TG)]).then_inc(ix_ready, 1)
                    pool.wait_ge(ix_ready, g + 1)
                    at_least(pool, xs_ready, g - 1)
                    at_least(pool, xsum_done, g - 1)
                    pool.sem_inc(gathers_begun, 1)
                    for t in range(TG):
                        pool.indirect_dma_start(out=xe[b][:, t, :], out_offset=None, in_=table,
                                                in_offset=bass.IndirectOffsetOnAxis(ap=ix[b][:, t:t + 1], axis=0))\
                            .then_inc(gathered[b], 16)

                over_groups(pool, step)
                pool.wait_ge(gathered[0], (NG - NG // 2) * 16 * TG)
                pool.wait_ge(gathered[1], (NG // 2) * 16 * TG)

            @block.scalar
            def _(act):
                def step(g, b, half):
                    if with_mlp:
                        for n in range(5):
                            if n < 4:
                                i = g * 4 + n
                                act.wait_ge(mm1_done, i + 1)
                                at_least(act, mm2_done, i - 1)
                                nc.scalar.activation(h1[n % 2][:, :], ps_1[:, :], ACT.Gelu_apprx_tanh,
                                                     bias=b1[:, :]).then_inc(h1_ready, 1)
                            if n > 0:
                                i, m = g * 4 + (n - 1), n - 1
                                act.wait_ge(mm2_done, i + 1)
                                at_least(act, h2_turned, i - 1)
                                nc.scalar.activation(h2T[m % 2][:, :], ps_2[:, :], ACT.Gelu_apprx_tanh,
                                                     bias=b2[:, :]).then_inc(h2T_ready, 1)
                    at_least(act, slot_done, g - 1)
                    for j in range(4):
                        act.wait_ge(g_done, g * 4 + (j + 1))
                        nc.scalar.copy(g_sb[b][:, 4 * j:4 * j + 4, :, :].rearrange("k t s i -> k (t s i)"),
                                       ps_g[j % 2][:, :]).then_inc(g_copied, 1)
                    act.wait_ge(xsum_done, g + 1)
                    at_least(act, slot_done, g)
                    nc.scalar.copy(xsum[:, :], ps_xsum).then_inc(xsum_copied, 1)

                over_groups(act, step)

            @block.vector
            def _(dve):
                steps = 5

                def spread_slots(g, b):
                    at_least(dve, scattered, g - 1)
                    nc.vector.tensor_scalar(hot_hi[b][:, :], his, node_hi[:, bass.ds(g, 1)], None, ALU.is_equal)
                    at_least(dve, spread_ready, g)
                    nc.vector.tensor_scalar(hot_lo[:, :], los, node_lo[:, bass.ds(g, 1)], None,
                                            ALU.is_equal).then_inc(hot_ready, 1)
                    dve.wait_ge(slot_done, g + 1)
                    nc.vector.tensor_copy(part[0][:, :], bank[3][:, 0:LAT + 1]).then_inc(split_step, 1)
                    dve.wait_ge(split_step, g * steps + 1)
                    nc.vector.tensor_tensor(left[0][:, :], ps_slot, part[0][:, 0:LAT], ALU.subtract)\
                        .then_inc(split_step, 1)
                    dve.wait_ge(split_step, g * steps + 2)
                    nc.vector.tensor_copy(part[1][:, 0:LAT], left[0][:, :]).then_inc(split_step, 1)
                    dve.wait_ge(split_step, g * steps + 3)
                    nc.vector.tensor_tensor(left[1][:, :], left[0][:, :], part[1][:, 0:LAT], ALU.subtract)\
                        .then_inc(split_step, 1)
                    dve.wait_ge(split_step, g * steps + 4)
                    nc.vector.tensor_copy(part[2][:, 0:LAT], left[1][:, :]).then_inc(split_step, 1)
                    dve.wait_ge(split_step, g * steps + 5)
                    dve.wait_ge(hot_ready, g + 1)
                    for s in range(3):
                        nc.vector.tensor_tensor(
                            spread[b][:, s, 0:NL].rearrange("p (l o) -> p l o", o=LAT),
                            hot_lo[:, :].unsqueeze(2).to_broadcast([P, LO, LAT]),
                            part[s][:, 0:LAT].unsqueeze(1).to_broadcast([P, LO, LAT]), ALU.mult)
                    nc.vector.tensor_tensor(spread[b][:, 0, NL:NLD], hot_lo[:, :],
                                            part[0][:, LAT:LAT + 1].to_broadcast([P, LO]), ALU.mult)\
                        .then_inc(spread_ready, 1)

                def step(g, b, half):
                    first = isinstance(g, int) and g == 0
                    if with_mlp:
                        dve.wait_ge(attr_turned, g + 1)
                        at_least(dve, mm1_done, g * 4)
                        nc.vector.tensor_copy(attrT[:, :], ps_attr[:, :]).then_inc(attrT_ready, 1)
                    if not first:
                        spread_slots(g - 1, 1 - b)
                    if with_mlp:
                        at_least(dve, g_done, 4 * (g - 1))
                        at_least(dve, h2_stored[b], half * 16)
                        for j in range(4):
                            dve.wait_ge(h2_turned, g * 4 + (j + 1))
                            nc.vector.tensor_copy(
                                h2[b][:, :, :].rearrange("p (q j) k -> p j q k", j=4)[:, j, :, :],
                                ps_t[:, :].rearrange("p (q k) -> p q k", k=K)).then_inc(h2_ready, 1)
                    at_least(dve, xsum_done, g - 1)
                    at_least(dve, g_done, 4 * (g - 1))
                    nc.vector.tensor_tensor(in_slot[b][:, :, :],
                                            rel[:, bass.ds(g * TG, TG)].unsqueeze(2).to_broadcast([P, TG, SL]),
                                            slots.unsqueeze(1).to_broadcast([P, TG, SL]), ALU.is_equal)\
                        .then_inc(in_slot_ready, 1)
                    dve.wait_ge(in_slot_ready, g + 1)
                    dve.wait_ge(gathered[b], half * (16 * TG) + 16 * TG)
                    for q in range(4):
                        t = slice(4 * q, 4 * q + 4)
                        last = nc.vector.tensor_tensor(
                            xs[b][:, t, :, :],
                            xe[b][:, t, :].unsqueeze(2).to_broadcast([P, 4, SL, LAT]),
                            in_slot[b][:, t, :].unsqueeze(3).to_broadcast([P, 4, SL, LAT]), ALU.mult)
                    last.then_inc(xs_ready, 1)

                over_groups(dve, step)
                spread_slots(NG - 1, 0)
                dve.wait_ge(scattered, NG)
                nc.vector.tensor_tensor(agg[0:HI, :], agg[0:HI, :], ps_agg[0:HI, 0:NLD], ALU.add)

            @block.tensor
            def _(pe):
                def mlp(g, b, half):
                    if isinstance(g, int) and g == NG - 1:
                        pe.wait_ge(attr_loaded[b], half * 16 + last_loads)
                    else:
                        pe.wait_ge(attr_loaded[b], half * 16 + 16)
                    at_least(pe, attrT_ready, g)
                    at_least(pe, xsum_copied, g)
                    for q in range(4):
                        last = nc.tensor.transpose(ps_attr[:, P * q:P * (q + 1)],
                                                   attr[b][:, 4 * q:4 * q + 4, :].rearrange("p t f -> p (t f)"), ident)
                    last.then_inc(attr_turned, 1)
                    pe.wait_ge(attrT_ready, g + 1)
                    for n in range(6):
                        if n < 4:
                            i = g * 4 + n
                            at_least(pe, h1_ready, i)
                            nc.tensor.matmul(ps_1[:, :], w1[32 * n:32 * n + ED, :], attrT[32 * n:32 * n + ED, :],
                                             start=True, stop=True).then_inc(mm1_done, 1)
                        if 1 <= n < 5:
                            i, m = g * 4 + (n - 1), n - 1
                            pe.wait_ge(h1_ready, i + 1)
                            at_least(pe, h2T_ready, i)
                            nc.tensor.matmul(ps_2[:, :], w2[:, :], h1[m % 2][:, :],
                                             start=True, stop=True).then_inc(mm2_done, 1)
                        if n >= 2:
                            i, m = g * 4 + (n - 2), n - 2
                            pe.wait_ge(h2T_ready, i + 1)
                            at_least(pe, h2_ready, i)
                            for q in range(4):
                                last = nc.tensor.transpose(ps_t[:, P * q:P * (q + 1)],
                                                           h2T[m % 2][:, P * q:P * (q + 1)], ident)
                            last.then_inc(h2_turned, 1)

                def scatter(g, b):
                    pe.wait_ge(spread_ready, g + 1)
                    known = isinstance(g, int)
                    for s in range(3):
                        n = NLD if s == 0 else NL
                        last = nc.tensor.matmul(ps_agg[0:HI, 0:n], hot_hi[b][:, :], spread[b][:, s, 0:n],
                                                start=known and g == 0 and s == 0,
                                                stop=known and g == NG - 1 and s == 2)
                    last.then_inc(scattered, 1)

                def step(g, b, half):
                    if with_mlp:
                        mlp(g, b, half)
                        pe.wait_ge(h2_ready, 4 * (g + 1))
                    else:
                        pe.wait_ge(h2_loaded[b], half * 16 + 16)
                    pe.wait_ge(xs_ready, g + 1)
                    for j in range(4):
                        at_least(pe, g_copied, g * 4 + (j - 1))
                        for t in range(4):
                            last = nc.tensor.matmul(ps_g[j % 2][:, P * t:P * (t + 1)], h2[b][:, 4 * j + t, :],
                                                    xs[b][:, 4 * j + t, :, :].rearrange("p s i -> p (s i)"),
                                                    start=True, stop=True)
                        last.then_inc(g_done, 1)
                    at_least(pe, xsum_copied, g)
                    for t in range(TG):
                        last = nc.tensor.matmul(ps_xsum[:, SL * t:SL * (t + 1)], xe[b][:, t, :], in_slot[b][:, t, :],
                                                start=True, stop=True)
                    last.then_inc(xsum_done, 1)
                    if not (isinstance(g, int) and g == 0):
                        scatter(g - 1, 1 - b)
                    at_least(pe, split_step, g * 5)
                    nc.tensor.matmul(ps_deg, in_slot[b][:, :, :].rearrange("p t s -> p (t s)"), ones[:, 0:1],
                                     start=True, stop=True)
                    pe.wait_ge(g_copied, g * 4 + 4)
                    for i in range(LAT):
                        nc.tensor.matmul(ps_slot, g_sb[b][:, :, :, i].rearrange("k t s -> k (t s)"), w3[:, LAT * i:LAT * (i + 1)],
                                         start=(i == 0), stop=False)
                    pe.wait_ge(xsum_copied, g + 1)
                    nc.tensor.matmul(ps_slot, xsum[:, :], b3[:, :], start=False, stop=True).then_inc(slot_done, 1)

                over_groups(pe, step)
                scatter(NG - 1, 0)

            block_ctx.__exit__(None, None, None)
            clear_counts()

        def update(layer):
            with nc.Block() as block:
                @block.vector
                def _(dve):
                    done = [0]

                    def link(ins):
                        done[0] += 1
                        ins.then_inc(s_chain, 1)
                        dve.wait_ge(s_chain, done[0])

                    nc.vector.tensor_copy(root_l[:, :], root[:, bass.ds(layer, 1), :].rearrange("p a c -> p (a c)"))
                    nc.vector.tensor_copy(rb_l[:, :], rb[:, bass.ds(layer, 1), :].rearrange("p a c -> p (a c)"))\
                        .then_inc(s_copied, 1)
                    for c in range(NCB):
                        n = min(CB, NL - c * CB)
                        dve.wait_ge(s_mm, c + 1)
                        nc.vector.tensor_copy(xT[0:n, c, :], bank[c % 2][0:n, 0:HI]).then_inc(s_copied, 1)
                    link(nc.vector.tensor_scalar(inv[0:HI, :], agg[0:HI, NL:NLD], 1.0, None, ALU.max))
                    link(nc.vector.reciprocal(inv[0:HI, :], inv[0:HI, :]))
                    link(nc.vector.tensor_tensor(pre[0:HI, :, :],
                                                 agg[0:HI, 0:NL].rearrange("p (l o) -> p l o", o=LAT),
                                                 inv[0:HI, :].unsqueeze(2).to_broadcast([HI, LO, LAT]), ALU.mult))
                    link(nc.vector.memset(agg[:, :], 0.0))
                    dve.wait_ge(s_mm, 2 * NCB)
                    link(nc.vector.tensor_tensor(pre[0:HI, :, :], pre[0:HI, :, :],
                                                 bank[2][0:HI, 0:NL].rearrange("p (l o) -> p l o", o=LAT), ALU.add))
                    dve.wait_ge(s_copied, 1)
                    link(nc.vector.tensor_tensor(pre[0:HI, :, :], pre[0:HI, :, :],
                                                 rb_l[0:HI, :].unsqueeze(1).to_broadcast([HI, LO, LAT]), ALU.add))

                @block.tensor
                def _(pe):
                    xn_f = xn[:, :, :].rearrange("p l f -> p (l f)")
                    for c in range(NCB):
                        n = min(CB, NL - c * CB)
                        if c >= 2:
                            pe.wait_ge(s_copied, c)
                        nc.tensor.transpose(bank[c % 2][0:n, 0:HI], xn_f[0:HI, c * CB:c * CB + n],
                                            ident[0:HI, 0:HI]).then_inc(s_mm, 1)
                    for c in range(NCB):
                        n = min(CB, NL - c * CB)
                        pe.wait_ge(s_copied, c + 2)
                        nc.tensor.matmul(bank[2][0:HI, c * CB:c * CB + n], xT[0:n, c, :], root_l[0:n, 0:n],
                                         start=True, stop=True).then_inc(s_mm, 1)

                @block.scalar
                def _(act):
                    act.wait_ge(s_chain, 6)
                    nc.scalar.activation(xn[0:HI, :, :], pre[0:HI, :, :], ACT.Gelu_apprx_tanh).then_inc(s_load, 1)

                @block.sync
                def _(sp):
                    sp.wait_ge(s_load, 1)
                    sp.dma_start(nodes_dram.rearrange("(h l) f -> h (l f)", l=LO),
                                 xn[0:HI, :, :].rearrange("p l f -> p (l f)")).then_inc(s_rows, 16)
                    sp.wait_ge(s_rows, 16)
            clear_counts()

        def finish():
            with nc.Block() as block:
                @block.vector
                def _(dve):
                    done = [0]

                    def link(ins):
                        done[0] += 1
                        ins.then_inc(s_chain, 1)
                        dve.wait_ge(s_chain, done[0])

                    y, m, v = pre[0:HI, :, :], mean[0:HI, :], var[0:HI, :]
                    wide3 = [HI, LO, LAT]
                    link(nc.vector.tensor_tensor(y, x0[0:HI, :, :], xn[0:HI, :, :], ALU.add))
                    link(nc.vector.tensor_reduce(m, y, AX.X, ALU.add))
                    link(nc.vector.tensor_scalar(m, m, 1.0 / LAT, None, ALU.mult))
                    link(nc.vector.tensor_tensor(y, y, m.unsqueeze(2).to_broadcast(wide3), ALU.subtract))
                    link(nc.vector.tensor_tensor(sq[0:HI, :, :], y, y, ALU.mult))
                    link(nc.vector.tensor_reduce(v, sq[0:HI, :, :], AX.X, ALU.add))
                    link(nc.vector.tensor_scalar(v, v, 1.0 / LAT, EPS, ALU.mult, ALU.add))
                    dve.wait_ge(s_mm, 1)
                    link(nc.vector.reciprocal(v, mean[0:HI, :]))
                    link(nc.vector.tensor_tensor(y, y, v.unsqueeze(2).to_broadcast(wide3), ALU.mult))

                @block.scalar
                def _(act):
                    act.wait_ge(s_chain, 7)
                    nc.scalar.activation(mean[0:HI, :], var[0:HI, :], ACT.Sqrt).then_inc(s_mm, 1)

                @block.sync
                def _(sp):
                    sp.wait_ge(s_chain, 9)
                    sp.dma_start(out.rearrange("(h l) f -> h (l f)", l=LO),
                                 pre[0:HI, :, :].rearrange("p l f -> p (l f)")).then_inc(s_rows, 16)
                    sp.wait_ge(s_rows, 16)

        ctx2 = ExitStack()
        with ctx2:
            setup()
        clear_counts()
        general = nc.values_load(flag[0:1, 0:1], min_val=0, max_val=RB * P)

        def other_windows(table):
            with nc.If(general > 0):
                with nc.Fori(1, NW):
                    windows("next")
                    edge_pass(table, False)
                windows("first")

        windows("first")
        edge_pass(x, True)
        other_windows(x)
        update(0)
        with nc.Fori(1, DEPTH) as layer:
            edge_pass(nodes_dram, False)
            other_windows(nodes_dram)
            update(layer)
        finish()


_INS = ['x', 'src', 'dst', 'edge_attr_6', 'L0_gnn_kW1', 'L0_gnn_kb1', 'L0_gnn_kW2', 'L0_gnn_kb2',
        'L0_gnn_kW3', 'L0_gnn_kb3', 'L0_gnn_root_W', 'L0_gnn_root_b']


def constant_table(n_nodes, n_edges, lat):
    import numpy as np
    d = layout(n_nodes, n_edges, lat)
    cols, n = constants(n_nodes, n_edges, lat)
    p = np.arange(P)
    table = np.zeros((P, n), np.float32)
    for name, v in (("ident", np.eye(P)),
                    ("slot_tile", p[:, None] // SL == np.arange(TG)[None]),
                    ("slot", (p % SL)[:, None]),
                    ("slots", np.arange(SL)[None]),
                    ("first_of_hi", d["LO"] * np.arange(d["HI"])[None]),
                    ("his", np.arange(d["HI"])[None]),
                    ("los", np.arange(d["LO"])[None])):
        table[:, cols[name][0]:cols[name][1]] = v
    return table


def kernel(**inputs):
    import numpy as np
    import concourse.bacc as bacc
    from concourse.bass_utils import run_bass_kernel_spmd

    nc = bacc.Bacc("TRN2", target_bir_lowering=False, num_devices=1)
    n, lat = inputs['x'].shape
    arrays, args = {}, []
    named = [(k, np.ascontiguousarray(inputs[k])) for k in _INS]
    named.append(("constants", constant_table(n, inputs['src'].shape[0], lat)))
    for name, a in named:
        arrays[f"in_{name}_dram"] = a
        args.append(nc.dram_tensor(f"in_{name}_dram", a.shape, mybir.dt.from_np(a.dtype), kind="ExternalInput").ap())
    out = nc.dram_tensor("out_0_dram", (n, lat), F32, kind="ExternalOutput").ap()
    gnn_kernel(nc, *args, out)
    r = run_bass_kernel_spmd(nc, [arrays], core_ids=[0])
    return r.results[0]["out_0_dram"]
```

```python
import concourse.bass as bass
from concourse import mybir
from contextlib import ExitStack

F32 = mybir.dt.float32
BF16 = mybir.dt.bfloat16
F16 = mybir.dt.float16
I32 = mybir.dt.int32
U32 = mybir.dt.uint32
ALU = mybir.AluOpType
ACT = mybir.ActivationFunctionType
AX = mybir.AxisListType

P = 128
TG = 16
SL = 8
PART = 9
NPICK = 6
BANK_PICKS = 3
QUAD = 32
MAGIC = 1.5 * 2 ** 23
NOWHERE = 1.0e6
EPS = 1e-5


def layout(n_nodes, n_edges, lat):
    lo = -(-n_nodes // P)
    hi = n_nodes // lo
    assert hi * lo == n_nodes and (lat + 1) * lo <= 512
    tiles = -(-n_edges // (P * TG)) * TG
    return dict(LO=lo, HI=hi, NT=tiles, NG=tiles // TG, RB=-(-tiles // P),
                NC=-(-n_nodes // (PART * P)))


def constants(n_nodes, n_edges, lat):
    d = layout(n_nodes, n_edges, lat)
    at, cols = 0, {}
    for name, n in (("ident", P), ("slot_tile", TG), ("slot", 1), ("slots", SL),
                    ("first_of_hi", d["HI"]), ("his", d["HI"]), ("los", d["LO"]),
                    ("parts", PART), ("chunk_hi", d["NC"]),
                    ("own_tile", 2 * P), ("fold", lat)):
        cols[name] = (at, at + n)
        at += n
    return cols, at


def at_least(eng, sem, value):
    if not isinstance(value, int) or value > 0:
        eng.wait_ge(sem, value)


def gnn_kernel(nc, x, src, dst, edge_attr, kW1, kb1, kW2, kb2, kW3, kb3, root_W, root_b, consts, out):
    N, LAT = x.shape
    E, ED = edge_attr.shape
    K = kW2.shape[0]
    DEPTH = root_W.shape[0]
    d = layout(N, E, LAT)
    LO, HI, NT, NG, RB = d["LO"], d["HI"], d["NT"], d["NG"], d["RB"]
    cols, ncols = constants(N, E, LAT)
    NW = -(-N // SL)
    FULL, REST = E // P, E % P
    NL = LO * LAT
    NLD = NL + LO
    PER = TG * LAT
    CB = 8 * LAT
    NCB = -(-NL // CB)
    NC = d["NC"]
    PL = PART * LAT
    PAIRS = (NG - 5) // 2
    assert NG % 2 == 1 and NG >= 7 and K == P and TG * SL == P

    nodes_dram = nc.dram_tensor("nodes_scratch", (N, LAT), F32).ap()
    part_dram = nc.dram_tensor("src_part_scratch", (NT, P), F16).ap()
    h2_dram = nc.dram_tensor("h2_scratch", (NG * P, TG * K), F32).ap()

    ctx = ExitStack()
    with ctx:
        def sb(name, shape, dt=F32):
            return ctx.enter_context(nc.sbuf_tensor(name, shape, dt))

        def sem(name):
            return ctx.enter_context(nc.semaphore(name))

        cst = sb("cst", [P, ncols])
        ident = cst[:, cols["ident"][0]:cols["ident"][1]]
        slot_tile = cst[:, cols["slot_tile"][0]:cols["slot_tile"][1]]
        slot = cst[:, cols["slot"][0]:cols["slot"][1]]
        slots = cst[:, cols["slots"][0]:cols["slots"][1]]
        first_of_hi = cst[:, cols["first_of_hi"][0]:cols["first_of_hi"][1]]
        his = cst[:, cols["his"][0]:cols["his"][1]]
        los = cst[:, cols["los"][0]:cols["los"][1]]
        parts = cst[:, cols["parts"][0]:cols["parts"][1]]
        chunk_hi = cst[:, cols["chunk_hi"][0]:cols["chunk_hi"][1]]
        own_tile = cst[:, cols["own_tile"][0]:cols["own_tile"][1]]
        fold = cst[:, cols["fold"][0]:cols["fold"][1]]
        ones = sb("ones", [P, P])
        w1 = sb("w1", [P, K])
        w2 = sb("w2", [K, K])
        w3 = sb("w3", [K, LAT, QUAD])
        b3 = sb("b3", [P, QUAD])
        b1 = sb("b1", [K, 1])
        b2 = sb("b2", [K, 1])
        root = sb("root", [P, DEPTH, P])
        rb = sb("rb", [P, DEPTH, LAT])
        rows_i = sb("rows_i", [P, 2, RB, P], I32)
        rows_f = sb("rows_f", [P, 2, RB, P])
        real = sb("real", [P, RB, P])
        least = sb("least", [P, RB])
        most = sb("most", [P, RB])
        wide = sb("wide", [P, RB])
        wide_any = sb("wide_any", [P, 1])
        narrow = sb("narrow", [P, 1])
        flag = sb("flag", [P, 1], I32)
        diag = sb("diag", [P, RB, P])
        src_e = sb("src_e", [P, NT], U32)
        src_f = sb("src_f", [P, NT])
        src_hi = sb("src_hi", [P, NT])
        src_part = sb("src_part", [P, NT])
        row_hi = sb("row_hi", [P, RB, P])
        row_hi16 = sb("row_hi16", [P, RB, P], F16)
        dst_e = sb("dst_e", [P, NT])
        base0 = sb("base0", [P, NT])
        base = sb("base", [P, NT])
        rel = sb("rel", [P, NT])
        picked = sb("picked", [P, NG, TG])
        node = sb("node", [P, NG])
        below = sb("below", [P, NG, HI])
        node_hi = sb("node_hi", [P, NG])
        node_lo = sb("node_lo", [P, NG])
        attr = [sb(f"attr{b}", [P, TG, 32]) for b in range(2)]
        attrT = sb("attrT", [P, 4 * P])
        h1 = [sb(f"h1_{b}", [K, 4 * P]) for b in range(2)]
        h2T = [sb(f"h2T_{b}", [K, 4 * P]) for b in range(2)]
        h2 = [sb(f"h2_{b}", [P, TG, K]) for b in range(2)]
        ix = [sb(f"ix{b}", [P, TG], U32) for b in range(2)]
        xe = [sb(f"xe{b}", [P, TG, LAT]) for b in range(2)]
        in_slot = [sb(f"in_slot{b}", [P, TG, SL]) for b in range(2)]
        hi_all = [sb(f"hi_all{b}", [P, NPICK * P], F16) for b in range(2)]
        hot_src = [sb(f"hot_src{b}", [P, NC, NPICK * P], BF16) for b in range(2)]
        hot_part = [sb(f"hot_part{b}", [P, NPICK, PART], BF16) for b in range(2)]
        masked = sb("masked", [P, NPICK, PART, LAT])
        table_f = sb("table_f", [P, NC, PL])
        table_left = sb("table_left", [P, NC, PL])
        table = sb("table", [P, NC, 3, PL], BF16)
        xs = [sb(f"xs{b}", [P, TG, SL, LAT]) for b in range(2)]
        g_sb = [sb(f"g_sb{b}", [K, TG, SL, LAT]) for b in range(2)]
        xsum = sb("xsum", [P, 2 * P])
        slotT = sb("slotT", [P, P])
        part = [sb(f"part{s}", [P, LAT + 1], BF16) for s in range(3)]
        left = [sb(f"left{s}", [P, LAT]) for s in range(2)]
        hot_hi = [sb(f"hot_hi{b}", [P, HI], BF16) for b in range(2)]
        hot_lo = sb("hot_lo", [P, LO], BF16)
        spread = [sb(f"spread{b}", [P, 3, NLD], BF16) for b in range(2)]
        x0 = sb("x0", [P, LO, LAT])
        xn = sb("xn", [P, LO, LAT])
        agg = sb("agg", [P, NLD])
        inv = sb("inv", [P, LO])
        xT = sb("xT", [P, NCB, HI])
        root_l = sb("root_l", [P, P])
        rb_l = sb("rb_l", [P, LAT])
        pre = sb("pre", [P, LO, LAT])
        mean = sb("mean", [P, LO])
        var = sb("var", [P, LO])
        sq = sb("sq", [P, LO, LAT])

        bank = [ctx.enter_context(nc.psum_tensor(f"bank{i}", [P, 512], F32)) for i in range(8)]
        ps_g = bank[0:2]
        ps_agg = bank[2]
        ps_slot = bank[3][:, 0:LAT]
        ps_deg = bank[3][:, LAT:LAT + 1]
        ps_slotT = bank[3][:, P:2 * P]
        ps_xsum = bank[4][:, 0:2 * P]
        ps_attr, ps_1, ps_2, ps_t = bank[4:8]
        ps_pick = bank[5:7]

        s_chain = sem("s_chain")
        s_load = sem("s_load")
        s_fill = sem("s_fill")
        s_rows = sem("s_rows")
        s_hi = sem("s_hi")
        s_hi_out = sem("s_hi_out")
        s_mm = sem("s_mm")
        s_copied = sem("s_copied")
        first_sem = [sem("attr_loaded0"), sem("attr_loaded1")]
        attr_loaded = first_sem
        attr_turned = sem("attr_turned")
        attrT_ready = sem("attrT_ready")
        mm1_done = sem("mm1_done")
        h1_ready = sem("h1_ready")
        mm2_done = sem("mm2_done")
        h2T_ready = sem("h2T_ready")
        h2_turned = sem("h2_turned")
        h2_ready = sem("h2_ready")
        h2_stored = [sem("h2_stored0"), sem("h2_stored1")]
        h2_loaded = [sem("h2_loaded0"), sem("h2_loaded1")]
        ix_ready = sem("ix_ready")
        gathers_begun = sem("gathers_begun")
        gathered = [sem("gathered0"), sem("gathered1")]
        in_slot_ready = sem("in_slot_ready")
        xs_ready = sem("xs_ready")
        hi_loaded = [sem("hi_loaded0"), sem("hi_loaded1")]
        hot_src_ready = sem("hot_src_ready")
        picked_done = sem("picked_done")
        masked_ready = sem("masked_ready")
        selected = sem("selected")
        g_done = sem("g_done")
        g_copied = sem("g_copied")
        xsum_done = sem("xsum_done")
        xsum_masked = sem("xsum_masked")
        slotT_done = sem("slotT_done")
        slotT_copied = sem("slotT_copied")
        slot_done = sem("slot_done")
        hot_ready = sem("hot_ready")
        split_step = sem("split_step")
        slot_read = sem("slot_read")
        spread_ready = sem("spread_ready")
        scattered = sem("scattered")
        agg_ready = sem("agg_ready")
        every = [s_chain, s_load, s_fill, s_rows, s_hi, s_hi_out, s_mm, s_copied, *attr_loaded, attr_turned, attrT_ready,
                 mm1_done, h1_ready, mm2_done, h2T_ready, h2_turned, h2_ready, *h2_stored, *h2_loaded,
                 ix_ready, gathers_begun, *gathered, in_slot_ready, xs_ready, *hi_loaded,
                 hot_src_ready, picked_done, masked_ready, selected, g_done, g_copied, xsum_done, xsum_masked,
                 slotT_done, slotT_copied,
                 slot_done, hot_ready, split_step, slot_read, spread_ready, scattered, agg_ready]

        def clear_counts():
            with nc.Block() as block:
                @block.gpsimd
                def _(pool):
                    pool.dma_reset()
                    for s in every:
                        pool.sem_clear(s)

        def setup():
            block = ctx2.enter_context(nc.Block())

            @block.sync
            def _(sp):
                sp.dma_start(cst[:, :], consts).then_inc(s_load, 16)
                sp.dma_start(w2[:, :], kW2).then_inc(s_load, 16)
                sp.dma_start(b1[:, :], kb1.rearrange("(k a) -> k a", a=1)).then_inc(s_load, 16)
                sp.dma_start(b2[:, :], kb2.rearrange("(k a) -> k a", a=1)).then_inc(s_load, 16)
                for j in range(4):
                    sp.dma_start(w1[32 * j:32 * j + ED, :], kW1).then_inc(s_load, 16)
                x_rows = x.rearrange("(h l) f -> h (l f)", l=LO)
                sp.dma_start(x0[0:HI, :, :].rearrange("p l f -> p (l f)"), x_rows).then_inc(s_load, 16)
                sp.dma_start(xn[0:HI, :, :].rearrange("p l f -> p (l f)"), x_rows).then_inc(s_load, 16)
                sp.dma_start(rb[:, :, :], root_b.rearrange("(a l) o -> a l o", a=1)
                             .to_broadcast([P, DEPTH, LAT])).then_inc(s_load, 16)
                sp.wait_ge(s_fill, 3)
                sp.dma_start(w3[:, :, 0:LAT], kW3.rearrange("k (i o) -> k i o", i=LAT)).then_inc(s_load, 16)
                for t in range(P // LAT):
                    sp.dma_start(b3[LAT * t:LAT * (t + 1), 0:LAT],
                                 kb3.rearrange("(i o) -> i o", i=LAT)).then_inc(s_load, 16)
                for q in range(8):
                    sp.dma_start(root[LAT * q:LAT * (q + 1), :, LAT * q:LAT * (q + 1)],
                                 root_W.rearrange("l i o -> i l o")).then_inc(s_load, 16)
                sp.wait_ge(s_fill, 5)
                for w, a in enumerate((src, dst)):
                    whole = FULL // P
                    if whole:
                        sp.dma_start(rows_i[:, w, 0:whole, :],
                                     a[0:whole * P * P].rearrange("(g r e) -> r g e", r=P, e=P)).then_inc(s_rows, 16)
                    more = FULL - whole * P
                    if more:
                        sp.dma_start(rows_i[0:more, w, whole, :],
                                     a[whole * P * P:FULL * P].rearrange("(r e) -> r e", e=P)).then_inc(s_rows, 16)
                    if REST:
                        sp.dma_start(rows_i[more:more + 1, w, whole, 0:REST],
                                     a[FULL * P:E].rearrange("(r e) -> r e", r=1)).then_inc(s_rows, 16)
                sp.wait_ge(s_hi, 1)
                whole, more = NT // P, NT % P
                sp.dma_start(part_dram[0:whole * P, :].rearrange("(g r) e -> r g e", r=P),
                             row_hi16[:, 0:whole, :]).then_inc(s_hi_out, 16) if whole else None
                if more:
                    sp.dma_start(part_dram[whole * P:NT, :], row_hi16[0:more, whole, :]).then_inc(s_hi_out, 16)
                sp.wait_ge(s_load, 16 * 28)
                sp.wait_ge(s_hi_out, 16 * (bool(whole) + bool(more)))

            n_rows = 16 * 2 * (bool(FULL // P) + bool(FULL % P) + bool(REST))

            @block.gpsimd
            def _(pool):
                pool.memset(root[:, :, :], 0.0).then_inc(s_fill, 1)
                pool.memset(w3[:, :, :], 0.0).then_inc(s_fill, 1)
                pool.memset(b3[:, :], 0.0).then_inc(s_fill, 1)
                pool.memset(rows_i[:, 0, :, :], 0).then_inc(s_fill, 1)
                pool.memset(rows_i[:, 1, :, :], int(NOWHERE)).then_inc(s_fill, 1)
                pool.memset(ones[:, :], 1.0).then_inc(s_fill, 1)
                for b in range(2):
                    pool.memset(attr[b][:, :, :], 0.0)
                pool.memset(agg[:, :], 0.0)
                pool.memset(table_f[:, :, :], 0.0)

            @block.vector
            def _(dve):
                done = [0]

                def link(ins):
                    done[0] += 1
                    ins.then_inc(s_chain, 1)
                    dve.wait_ge(s_chain, done[0])

                dve.wait_ge(s_load, 16 * 28)
                dve.wait_ge(s_rows, n_rows)
                link(nc.vector.tensor_copy(rows_f[:, :, :, :], rows_i[:, :, :, :]))
                def divide(hi, of):
                    link(nc.vector.tensor_scalar(hi, of, 1.0 / PART, -(PART - 1) / 2 / PART, ALU.mult, ALU.add))
                    link(nc.vector.tensor_scalar(hi, hi, MAGIC, None, ALU.add))
                    link(nc.vector.tensor_scalar(hi, hi, -MAGIC, None, ALU.add))

                divide(row_hi[:, :, :], rows_f[:, 0, :, :])
                nc.vector.tensor_copy(row_hi16[:, :, :], row_hi[:, :, :]).then_inc(s_hi, 1)
                link(nc.vector.tensor_reduce(least[:, :], rows_f[:, 1, :, :], AX.X, ALU.min))
                link(nc.vector.scalar_tensor_tensor(real[:, :, :], rows_f[:, 1, :, :], NOWHERE / 2,
                                                    rows_f[:, 1, :, :], ALU.is_lt, ALU.mult))
                link(nc.vector.tensor_reduce(most[:, :], real[:, :, :], AX.X, ALU.max))
                link(nc.vector.tensor_tensor(wide[:, :], most[:, :], least[:, :], ALU.subtract))
                link(nc.vector.tensor_scalar(wide[:, :], wide[:, :], float(SL - 1), None, ALU.is_gt))
                link(nc.vector.tensor_reduce(wide_any[:, :], wide[:, :], AX.X, ALU.add))
                for r in range(RB):
                    link(nc.vector.tensor_scalar(diag[:, r, :], ident, least[:, r:r + 1], None, ALU.mult))
                for r in range(RB):
                    n = min(P, NT - r * P)
                    at = slice(r * P, r * P + n)
                    dve.wait_ge(s_mm, r + 1)
                    nc.vector.tensor_copy(base0[:, at], bank[r % 2][:, 0:n])
                    nc.vector.tensor_copy(src_e[:, at], bank[r % 2][:, P:P + n])
                    nc.vector.tensor_copy(src_f[:, at], bank[r % 2][:, P:P + n])
                    nc.vector.tensor_copy(dst_e[:, at], bank[r % 2][:, 2 * P:2 * P + n]).then_inc(s_copied, 1)
                dve.wait_ge(s_mm, RB + 1)
                link(nc.vector.tensor_copy(flag[:, :], bank[2][:, 0:1]))
                link(nc.vector.tensor_scalar(narrow[:, :], bank[2][:, 0:1], 0.5, None, ALU.is_lt))
                link(nc.vector.tensor_scalar(base0[:, :], base0[:, :], narrow[:, :], None, ALU.mult))
                divide(src_hi[:, :], src_f[:, :])
                nc.vector.scalar_tensor_tensor(src_part[:, :], src_hi[:, :], -float(PART), src_f[:, :],
                                               ALU.mult, ALU.add)

            @block.tensor
            def _(pe):
                pe.wait_ge(s_fill, 6)
                pe.wait_ge(s_chain, 10 + RB)
                for r in range(RB):
                    if r >= 2:
                        pe.wait_ge(s_copied, r - 1)
                    nc.tensor.matmul(bank[r % 2][:, 0:P], ones[:, :], diag[:, r, :], start=True, stop=True)
                    nc.tensor.transpose(bank[r % 2][:, P:2 * P], rows_f[:, 0, r, :], ident)
                    nc.tensor.transpose(bank[r % 2][:, 2 * P:3 * P], rows_f[:, 1, r, :], ident).then_inc(s_mm, 1)
                nc.tensor.matmul(bank[2][:, 0:1], ones[:, :], wide_any[:, :], start=True, stop=True).then_inc(s_mm, 1)

        def windows(new_base):
            with nc.Block() as block:
                @block.vector
                def _(dve):
                    done = [0]

                    def link(ins):
                        done[0] += 1
                        ins.then_inc(s_chain, 1)
                        dve.wait_ge(s_chain, done[0])

                    if new_base == "first":
                        link(nc.vector.tensor_copy(base[:, :], base0[:, :]))
                    if new_base == "next":
                        link(nc.vector.tensor_scalar(base[:, :], base[:, :], float(SL), None, ALU.add))
                    link(nc.vector.tensor_tensor(rel[:, :], dst_e[:, :], base[:, :], ALU.subtract))
                    link(nc.vector.tensor_tensor(picked[:, :, :], base[:, :].rearrange("p (g t) -> p g t", t=TG),
                                                 slot_tile.unsqueeze(1).to_broadcast([P, NG, TG]), ALU.mult))
                    link(nc.vector.tensor_reduce(node[:, :], picked[:, :, :], AX.X, ALU.add))
                    link(nc.vector.tensor_scalar(node[:, :], node[:, :], slot, None, ALU.add))
                    link(nc.vector.tensor_tensor(below[:, :, :], node[:, :].unsqueeze(2).to_broadcast([P, NG, HI]),
                                                 first_of_hi.unsqueeze(1).to_broadcast([P, NG, HI]), ALU.is_ge))
                    link(nc.vector.tensor_reduce(node_hi[:, :], below[:, :, :], AX.X, ALU.add))
                    link(nc.vector.tensor_scalar(node_hi[:, :], node_hi[:, :], -1.0, None, ALU.add))
                    link(nc.vector.scalar_tensor_tensor(node_lo[:, :], node_hi[:, :], -float(LO), node[:, :],
                                                        ALU.mult, ALU.add))
            clear_counts()

        def edge_pass(rows, with_mlp):
            n_pick = 0 if with_mlp else NPICK
            n_banks = n_pick // BANK_PICKS
            n_dma = TG - n_pick
            block_ctx = nc.Block()
            block = block_ctx.__enter__()

            def over_groups(eng, step):
                step(0, 0, 0)
                step(1, 1, 0)
                with eng.Fori(1, 1 + PAIRS) as h:
                    step(h * 2, 0, h)
                    step(h * 2 + 1, 1, h)
                for g in range(NG - 3, NG):
                    step(g, g % 2, g // 2)

            def last_group(g):
                return isinstance(g, int) and g == NG - 1

            @block.sync
            def _(sp):
                def store(g, b):
                    sp.wait_ge(h2_ready, 4 * (g + 1))
                    sp.dma_start(h2_dram[bass.ds(g * P, P), :], h2[b][:, :, :].rearrange("p t k -> p (t k)"))\
                      .then_inc(h2_stored[b], 16)

                def load_hi(g, b):
                    at_least(sp, hot_src_ready, g - 1)
                    sp.dma_start(hi_all[b][:, :], part_dram[bass.ds(g * TG + n_dma, n_pick), :]
                                 .rearrange("t e -> (t e)").unsqueeze(0).to_broadcast([P, n_pick * P]))\
                      .then_inc(hi_loaded[b], 16)

                def step(g, b, half):
                    if not with_mlp:
                        if not last_group(g):
                            load_hi(g + 1, 1 - b)
                        at_least(sp, g_done, 4 * (g - 1))
                        sp.dma_start(h2[b][:, :, :].rearrange("p t k -> p (t k)"),
                                     h2_dram[bass.ds(g * P, P), :]).then_inc(h2_loaded[b], 16)
                        return
                    at_least(sp, attr_turned, g - 1)
                    if last_group(g):
                        t = FULL - g * TG
                        if t:
                            sp.dma_start(attr[b][:, 0:t, 0:ED], edge_attr[g * TG * P:FULL * P, :]
                                         .rearrange("(t e) f -> e t f", e=P)).then_inc(attr_loaded[b], 16)
                        if REST:
                            sp.dma_start(attr[b][0:REST, t, 0:ED], edge_attr[FULL * P:E, :]).then_inc(attr_loaded[b], 16)
                    else:
                        sp.dma_start(attr[b][:, :, 0:ED], edge_attr[bass.ds(g * (TG * P), TG * P), :]
                                     .rearrange("(t e) f -> e t f", e=P)).then_inc(attr_loaded[b], 16)
                    if not isinstance(g, int) or g >= 1:
                        store(g - 1, 1 - b)

                if not with_mlp:
                    load_hi(0, 0)
                over_groups(sp, step)
                if with_mlp:
                    store(NG - 1, 0)
                    sp.wait_ge(h2_stored[0], 16 * (NG - NG // 2))
                    sp.wait_ge(h2_stored[1], 16 * (NG // 2))

            last_loads = 16 * (bool(FULL - (NG - 1) * TG) + bool(REST))

            @block.gpsimd
            def _(pool):
                def step(g, b, half):
                    at_least(pool, gathered[b], half * (16 * n_dma))
                    nc.gpsimd.tensor_copy(ix[b][:, :], src_e[:, bass.ds(g * TG, TG)]).then_inc(ix_ready, 1)
                    pool.wait_ge(ix_ready, g + 1)
                    at_least(pool, xs_ready, g - 1)
                    at_least(pool, xsum_done, g - 1)
                    pool.sem_inc(gathers_begun, 1)
                    for t in range(n_dma):
                        pool.indirect_dma_start(out=xe[b][:, t, :], out_offset=None, in_=rows,
                                                in_offset=bass.IndirectOffsetOnAxis(ap=ix[b][:, t:t + 1], axis=0))\
                            .then_inc(gathered[b], 16)

                over_groups(pool, step)
                pool.wait_ge(gathered[0], (NG - NG // 2) * 16 * n_dma)
                pool.wait_ge(gathered[1], (NG // 2) * 16 * n_dma)

            @block.scalar
            def _(act):
                def hidden1(g, n):
                    act.wait_ge(mm1_done, g * 4 + (n + 1))
                    at_least(act, mm2_done, g * 4 + (n - 1))
                    nc.scalar.activation(h1[n % 2][:, :], ps_1[:, :], ACT.Gelu_apprx_tanh,
                                         bias=b1[:, :]).then_inc(h1_ready, 1)

                def hidden2(g, n):
                    act.wait_ge(mm2_done, g * 4 + (n + 1))
                    at_least(act, h2_turned, g * 4 + (n - 1))
                    nc.scalar.activation(h2T[n % 2][:, :], ps_2[:, :], ACT.Gelu_apprx_tanh,
                                         bias=b2[:, :]).then_inc(h2T_ready, 1)

                def copy_g(g, b, j):
                    act.wait_ge(g_done, g * 4 + (j + 1))
                    nc.scalar.copy(g_sb[b][:, 4 * j:4 * j + 4, :, :].rearrange("k t s i -> k (t s i)"),
                                   ps_g[j % 2][:, :]).then_inc(g_copied, 1)

                def step(g, b, half):
                    more = with_mlp and not last_group(g)
                    at_least(act, slotT_done, g - 1)
                    for j in range(4):
                        copy_g(g, b, j)
                        if more:
                            hidden1(g + 1, j)
                            if j:
                                hidden2(g + 1, j - 1)
                    if more:
                        hidden2(g + 1, 3)
                    act.wait_ge(slotT_done, g + 1)
                    at_least(act, slot_done, g)
                    nc.scalar.copy(slotT[:, :], ps_slotT).then_inc(slotT_copied, 1)

                if with_mlp:
                    for n in range(5):
                        if n < 4:
                            hidden1(0, n)
                        if n:
                            hidden2(0, n - 1)
                over_groups(act, step)

            @block.vector
            def _(dve):
                steps = 5

                def spread_slots(g, b):
                    at_least(dve, scattered, g - 1)
                    nc.vector.tensor_scalar(hot_hi[b][:, :], his, node_hi[:, bass.ds(g, 1)], None, ALU.is_equal)
                    at_least(dve, spread_ready, g)
                    nc.vector.tensor_scalar(hot_lo[:, :], los, node_lo[:, bass.ds(g, 1)], None,
                                            ALU.is_equal).then_inc(hot_ready, 1)
                    dve.wait_ge(slot_done, g + 1)
                    nc.vector.tensor_copy(part[0][:, :], bank[3][:, 0:LAT + 1]).then_inc(split_step, 1)
                    dve.wait_ge(split_step, g * steps + 1)
                    nc.vector.tensor_tensor(left[0][:, :], ps_slot, part[0][:, 0:LAT], ALU.subtract)\
                        .then_inc(split_step, 1)
                    dve.wait_ge(split_step, g * steps + 2)
                    nc.vector.tensor_copy(part[1][:, 0:LAT], left[0][:, :]).then_inc(split_step, 1)
                    dve.wait_ge(split_step, g * steps + 3)
                    nc.vector.tensor_tensor(left[1][:, :], left[0][:, :], part[1][:, 0:LAT], ALU.subtract)\
                        .then_inc(split_step, 1)
                    dve.wait_ge(split_step, g * steps + 4)
                    nc.vector.tensor_copy(part[2][:, 0:LAT], left[1][:, :]).then_inc(split_step, 1)
                    dve.wait_ge(split_step, g * steps + 5)
                    dve.wait_ge(hot_ready, g + 1)
                    for s in range(3):
                        nc.vector.tensor_tensor(
                            spread[b][:, s, 0:NL].rearrange("p (l o) -> p l o", o=LAT),
                            hot_lo[:, :].unsqueeze(2).to_broadcast([P, LO, LAT]),
                            part[s][:, 0:LAT].unsqueeze(1).to_broadcast([P, LO, LAT]), ALU.mult)
                    nc.vector.tensor_tensor(spread[b][:, 0, NL:NLD], hot_lo[:, :],
                                            part[0][:, LAT:LAT + 1].to_broadcast([P, LO]), ALU.mult)\
                        .then_inc(spread_ready, 1)

                def copy_attr(g):
                    dve.wait_ge(attr_turned, g + 1)
                    at_least(dve, mm1_done, g * 4)
                    nc.vector.tensor_copy(attrT[:, :], ps_attr[:, :]).then_inc(attrT_ready, 1)

                def copy_h2(g, b, half, quarters):
                    at_least(dve, g_done, 4 * (g - 1))
                    at_least(dve, h2_stored[b], half * 16)
                    for j in quarters:
                        dve.wait_ge(h2_turned, g * 4 + (j + 1))
                        nc.vector.tensor_copy(
                            h2[b][:, :, :].rearrange("p (q j) k -> p j q k", j=4)[:, j, :, :],
                            ps_t[:, :].rearrange("p (q k) -> p q k", k=K)).then_inc(h2_ready, 1)

                def hot_sources(g, b, half):
                    at_least(dve, picked_done, (g - 1) * n_banks)
                    at_least(dve, selected, (g - 1) * n_banks)
                    nc.vector.tensor_tensor(
                        hot_part[b][:, :, :],
                        src_part[:, bass.ds(g * TG + n_dma, n_pick)].unsqueeze(2).to_broadcast([P, n_pick, PART]),
                        parts.unsqueeze(1).to_broadcast([P, n_pick, PART]), ALU.is_equal)
                    dve.wait_ge(hi_loaded[b], half * 16 + 16)
                    for c in range(NC):
                        last = nc.vector.tensor_scalar(hot_src[b][:, c, :], hi_all[b][:, :], chunk_hi[:, c:c + 1],
                                                       None, ALU.is_equal)
                    last.then_inc(hot_src_ready, 1)

                def select(g, b, half):
                    at_least(dve, xsum_done, g - 1)
                    dve.wait_ge(hot_src_ready, g + 1)
                    for j in range(n_banks):
                        t = slice(BANK_PICKS * j, BANK_PICKS * (j + 1))
                        dve.wait_ge(picked_done, g * n_banks + (j + 1))
                        at_least(dve, selected, (g - 1) * n_banks + (j + 1))
                        nc.vector.tensor_tensor(
                            masked[:, t, :, :],
                            ps_pick[j][:, 0:BANK_PICKS * PL].rearrange("p (t l f) -> p t l f", t=BANK_PICKS, l=PART),
                            hot_part[b][:, t, :].unsqueeze(3).to_broadcast([P, BANK_PICKS, PART, LAT]), ALU.mult)\
                            .then_inc(masked_ready, 1)
                        dve.wait_ge(masked_ready, g * n_banks + (j + 1))
                        nc.vector.tensor_reduce(xe[b][:, n_dma + BANK_PICKS * j:n_dma + BANK_PICKS * (j + 1), :],
                                                masked[:, t, :, :].rearrange("p t l f -> p t f l"), AX.X, ALU.add)\
                            .then_inc(selected, 1)

                def slot_products(g, b, half):
                    at_least(dve, slotT_done, g - 1)
                    at_least(dve, g_done, 4 * (g - 1))
                    nc.vector.tensor_tensor(in_slot[b][:, :, :],
                                            rel[:, bass.ds(g * TG, TG)].unsqueeze(2).to_broadcast([P, TG, SL]),
                                            slots.unsqueeze(1).to_broadcast([P, TG, SL]), ALU.is_equal)\
                        .then_inc(in_slot_ready, 1)
                    dve.wait_ge(in_slot_ready, g + 1)
                    dve.wait_ge(gathered[b], half * (16 * n_dma) + 16 * n_dma)
                    if n_pick:
                        dve.wait_ge(selected, (g + 1) * n_banks)
                    for q in range(4):
                        t = slice(4 * q, 4 * q + 4)
                        last = nc.vector.tensor_tensor(
                            xs[b][:, t, :, :],
                            xe[b][:, t, :].unsqueeze(2).to_broadcast([P, 4, SL, LAT]),
                            in_slot[b][:, t, :].unsqueeze(3).to_broadcast([P, 4, SL, LAT]), ALU.mult)
                    last.then_inc(xs_ready, 1)

                def mask_xsum(g):
                    at_least(dve, slotT_done, g)
                    dve.wait_ge(xsum_done, g + 1)
                    nc.vector.tensor_tensor(xsum[:, :], ps_xsum, own_tile, ALU.mult).then_inc(xsum_masked, 1)

                def step(g, b, half):
                    nxt = (g + 1, 1 - b, half + b)
                    more = not last_group(g)
                    if with_mlp and more:
                        copy_attr(g + 1)
                    if not (isinstance(g, int) and g == 0):
                        spread_slots(g - 1, 1 - b)
                    mask_xsum(g)
                    if n_pick and (not isinstance(g, int) or g + 3 < NG):
                        hot_sources(g + 3, 1 - b, half + b + 1)
                    if with_mlp and more:
                        copy_h2(*nxt, (0, 1))
                    if more:
                        slot_products(*nxt)
                    if with_mlp and more:
                        copy_h2(*nxt, (2, 3))
                    if n_pick and (not isinstance(g, int) or g + 2 < NG):
                        select(g + 2, b, half + 1)

                if with_mlp:
                    copy_attr(0)
                    copy_h2(0, 0, 0, range(4))
                if n_pick:
                    hot_sources(0, 0, 0)
                    hot_sources(1, 1, 0)
                    select(0, 0, 0)
                    hot_sources(2, 0, 1)
                    select(1, 1, 0)
                slot_products(0, 0, 0)
                over_groups(dve, step)
                spread_slots(NG - 1, 0)
                dve.wait_ge(scattered, NG)
                nc.vector.tensor_tensor(agg[0:HI, :], agg[0:HI, :], ps_agg[0:HI, 0:NLD], ALU.add)

            @block.tensor
            def _(pe):
                def turn_attr(g, b, half):
                    if last_group(g):
                        pe.wait_ge(attr_loaded[b], half * 16 + last_loads)
                    else:
                        pe.wait_ge(attr_loaded[b], half * 16 + 16)
                    at_least(pe, attrT_ready, g)
                    at_least(pe, xsum_masked, g - 1)
                    for q in range(4):
                        last = nc.tensor.transpose(ps_attr[:, P * q:P * (q + 1)],
                                                   attr[b][:, 4 * q:4 * q + 4, :].rearrange("p t f -> p (t f)"), ident)
                    last.then_inc(attr_turned, 1)

                def product1(g, n):
                    if n == 0:
                        pe.wait_ge(attrT_ready, g + 1)
                    at_least(pe, h1_ready, g * 4 + n)
                    nc.tensor.matmul(ps_1[:, :], w1[32 * n:32 * n + ED, :], attrT[32 * n:32 * n + ED, :],
                                     start=True, stop=True).then_inc(mm1_done, 1)

                def product2(g, n):
                    pe.wait_ge(h1_ready, g * 4 + (n + 1))
                    at_least(pe, h2T_ready, g * 4 + n)
                    nc.tensor.matmul(ps_2[:, :], w2[:, :], h1[n % 2][:, :],
                                     start=True, stop=True).then_inc(mm2_done, 1)

                def turn_h2(g, n):
                    pe.wait_ge(h2T_ready, g * 4 + (n + 1))
                    at_least(pe, h2_ready, g * 4 + n)
                    for q in range(4):
                        last = nc.tensor.transpose(ps_t[:, P * q:P * (q + 1)],
                                                   h2T[n % 2][:, P * q:P * (q + 1)], ident)
                    last.then_inc(h2_turned, 1)

                def scatter(g, b):
                    pe.wait_ge(spread_ready, g + 1)
                    known = isinstance(g, int)
                    for s in range(3):
                        n = NLD if s == 0 else NL
                        last = nc.tensor.matmul(ps_agg[0:HI, 0:n], hot_hi[b][:, :], spread[b][:, s, 0:n],
                                                start=known and g == 0 and s == 0,
                                                stop=known and g == NG - 1 and s == 2)
                    last.then_inc(scattered, 1)

                def pick(g, b):
                    pe.wait_ge(hot_src_ready, g + 1)
                    for j in range(n_banks):
                        at_least(pe, selected, (g - 1) * n_banks + (j + 1))
                        for t in range(BANK_PICKS):
                            e = (BANK_PICKS * j + t) * P
                            for c in range(NC):
                                for s in range(3):
                                    last = nc.tensor.matmul(ps_pick[j][:, PL * t:PL * (t + 1)],
                                                            hot_src[b][:, c, e:e + P], table[:, c, s, :],
                                                            start=(c == 0 and s == 0), stop=(c == NC - 1 and s == 2))
                        last.then_inc(picked_done, 1)

                def sum_tiles(g, b, j):
                    at_least(pe, g_copied, g * 4 + (j - 1))
                    for t in range(4):
                        last = nc.tensor.matmul(ps_g[j % 2][:, P * t:P * (t + 1)], h2[b][:, 4 * j + t, :],
                                                xs[b][:, 4 * j + t, :, :].rearrange("p s i -> p (s i)"),
                                                start=True, stop=True)
                    last.then_inc(g_done, 1)

                def sum_x(g, b):
                    at_least(pe, xsum_masked, g)
                    if with_mlp and not last_group(g):
                        pe.wait_ge(attrT_ready, g + 2)
                    for h in range(2):
                        last = nc.tensor.matmul(ps_xsum[:, P * h:P * (h + 1)],
                                                xe[b][:, TG // 2 * h:TG // 2 * (h + 1), :].rearrange("p t f -> p (t f)"),
                                                in_slot[b][:, :, :].rearrange("p t s -> p (t s)"),
                                                start=True, stop=True)
                    last.then_inc(xsum_done, 1)

                def slot_messages(g, b):
                    at_least(pe, spread_ready, g)
                    nc.tensor.matmul(ps_deg, in_slot[b][:, :, :].rearrange("p t s -> p (t s)"), ones[:, 0:1],
                                     start=True, stop=True)
                    pe.wait_ge(g_copied, g * 4 + 4)
                    for i in range(LAT):
                        c = i % 4
                        nc.tensor.matmul(ps_slotT[QUAD * c:QUAD * (c + 1), :], w3[:, i, :],
                                         g_sb[b][:, :, :, i].rearrange("k t s -> k (t s)"),
                                         start=(i < 4), stop=(i >= LAT - 2))
                    pe.wait_ge(xsum_masked, g + 1)
                    for h in range(2):
                        last = nc.tensor.matmul(ps_slotT[QUAD * h:QUAD * (h + 1), :], b3[:, :],
                                                xsum[:, P * h:P * (h + 1)], start=False, stop=True)
                    last.then_inc(slotT_done, 1)

                def fold_slots(g):
                    pe.wait_ge(slotT_copied, g + 1)
                    nc.tensor.matmul(ps_slot, slotT[:, :], fold, start=True, stop=True).then_inc(slot_done, 1)

                def step(g, b, half):
                    nxt = g + 1
                    more = with_mlp and not last_group(g)
                    if not (isinstance(g, int) and g == 0):
                        fold_slots(g - 1)
                    if more:
                        turn_attr(nxt, 1 - b, half + b)
                    if with_mlp:
                        pe.wait_ge(h2_ready, 4 * (g + 1))
                    else:
                        pe.wait_ge(h2_loaded[b], half * 16 + 16)
                    pe.wait_ge(xs_ready, g + 1)
                    for j in range(4):
                        sum_tiles(g, b, j)
                        if j == 0:
                            sum_x(g, b)
                        if more:
                            product1(nxt, j)
                            if j >= 1:
                                product2(nxt, j - 1)
                            if j >= 2:
                                turn_h2(nxt, j - 2)
                    if more:
                        product2(nxt, 3)
                        turn_h2(nxt, 2)
                    if n_pick and (not isinstance(g, int) or g + 2 < NG):
                        pick(g + 2, b)
                    if not (isinstance(g, int) and g == 0):
                        scatter(g - 1, 1 - b)
                    if more:
                        turn_h2(nxt, 3)
                    slot_messages(g, b)

                if with_mlp:
                    turn_attr(0, 0, 0)
                    for n in range(6):
                        if n < 4:
                            product1(0, n)
                        if 1 <= n < 5:
                            product2(0, n - 1)
                        if n >= 2:
                            turn_h2(0, n - 2)
                if n_pick:
                    pick(0, 0)
                    pick(1, 1)
                over_groups(pe, step)
                fold_slots(NG - 1)
                scatter(NG - 1, 0)

            block_ctx.__exit__(None, None, None)
            clear_counts()

        hi_rows, hi_rest = N // PART, N % PART
        n_table = bool(hi_rows // P) + bool(hi_rows % P) + bool(hi_rest)

        def load_table(sp, nodes):
            whole, more = hi_rows // P, hi_rows % P
            if whole:
                sp.dma_start(table_f[:, 0:whole, :], nodes[0:whole * P * PART, :]
                             .rearrange("(c p l) f -> p c (l f)", p=P, l=PART)).then_inc(s_rows, 16)
            if more:
                sp.dma_start(table_f[0:more, whole, :], nodes[whole * P * PART:hi_rows * PART, :]
                             .rearrange("(p l) f -> p (l f)", l=PART)).then_inc(s_rows, 16)
            if hi_rest:
                sp.dma_start(table_f[more:more + 1, whole, 0:hi_rest * LAT], nodes[hi_rows * PART:N, :]
                             .rearrange("(p l) f -> p (l f)", p=1)).then_inc(s_rows, 16)

        def split_table(dve, link, loaded):
            dve.wait_ge(s_rows, loaded)
            of = table_f[:, :, :]
            for s in range(3):
                link(nc.vector.tensor_copy(table[:, :, s, :], of))
                if s < 2:
                    link(nc.vector.tensor_tensor(table_left[:, :, :], of, table[:, :, s, :], ALU.subtract))
                    of = table_left[:, :, :]

        def update(layer):
            with nc.Block() as block:
                @block.vector
                def _(dve):
                    done = [0]

                    def link(ins):
                        done[0] += 1
                        ins.then_inc(s_chain, 1)
                        dve.wait_ge(s_chain, done[0])

                    nc.vector.tensor_copy(root_l[:, :], root[:, bass.ds(layer, 1), :].rearrange("p a c -> p (a c)"))
                    nc.vector.tensor_copy(rb_l[:, :], rb[:, bass.ds(layer, 1), :].rearrange("p a c -> p (a c)"))\
                        .then_inc(s_copied, 1)
                    for c in range(NCB):
                        n = min(CB, NL - c * CB)
                        dve.wait_ge(s_mm, c + 1)
                        nc.vector.tensor_copy(xT[0:n, c, :], bank[c % 2][0:n, 0:HI]).then_inc(s_copied, 1)
                    link(nc.vector.tensor_scalar(inv[0:HI, :], agg[0:HI, NL:NLD], 1.0, None, ALU.max))
                    link(nc.vector.reciprocal(inv[0:HI, :], inv[0:HI, :]))
                    link(nc.vector.tensor_tensor(pre[0:HI, :, :],
                                                 agg[0:HI, 0:NL].rearrange("p (l o) -> p l o", o=LAT),
                                                 inv[0:HI, :].unsqueeze(2).to_broadcast([HI, LO, LAT]), ALU.mult))
                    link(nc.vector.memset(agg[:, :], 0.0))
                    dve.wait_ge(s_mm, 2 * NCB)
                    link(nc.vector.tensor_tensor(pre[0:HI, :, :], pre[0:HI, :, :],
                                                 bank[2][0:HI, 0:NL].rearrange("p (l o) -> p l o", o=LAT), ALU.add))
                    dve.wait_ge(s_copied, 1)
                    link(nc.vector.tensor_tensor(pre[0:HI, :, :], pre[0:HI, :, :],
                                                 rb_l[0:HI, :].unsqueeze(1).to_broadcast([HI, LO, LAT]), ALU.add))
                    split_table(dve, link, 16 + 16 * n_table)

                @block.tensor
                def _(pe):
                    xn_f = xn[:, :, :].rearrange("p l f -> p (l f)")
                    for c in range(NCB):
                        n = min(CB, NL - c * CB)
                        if c >= 2:
                            pe.wait_ge(s_copied, c)
                        nc.tensor.transpose(bank[c % 2][0:n, 0:HI], xn_f[0:HI, c * CB:c * CB + n],
                                            ident[0:HI, 0:HI]).then_inc(s_mm, 1)
                    for c in range(NCB):
                        n = min(CB, NL - c * CB)
                        pe.wait_ge(s_copied, c + 2)
                        nc.tensor.matmul(bank[2][0:HI, c * CB:c * CB + n], xT[0:n, c, :], root_l[0:n, 0:n],
                                         start=True, stop=True).then_inc(s_mm, 1)

                @block.scalar
                def _(act):
                    act.wait_ge(s_chain, 6)
                    nc.scalar.activation(xn[0:HI, :, :], pre[0:HI, :, :], ACT.Gelu_apprx_tanh).then_inc(s_load, 1)

                @block.sync
                def _(sp):
                    sp.wait_ge(s_load, 1)
                    sp.dma_start(nodes_dram.rearrange("(h l) f -> h (l f)", l=LO),
                                 xn[0:HI, :, :].rearrange("p l f -> p (l f)")).then_inc(s_rows, 16)
                    sp.wait_ge(s_rows, 16)
                    load_table(sp, nodes_dram)
                    sp.wait_ge(s_rows, 16 + 16 * n_table)
            clear_counts()

        def finish():
            with nc.Block() as block:
                @block.vector
                def _(dve):
                    done = [0]

                    def link(ins):
                        done[0] += 1
                        ins.then_inc(s_chain, 1)
                        dve.wait_ge(s_chain, done[0])

                    y, m, v = pre[0:HI, :, :], mean[0:HI, :], var[0:HI, :]
                    wide3 = [HI, LO, LAT]
                    link(nc.vector.tensor_tensor(y, x0[0:HI, :, :], xn[0:HI, :, :], ALU.add))
                    link(nc.vector.tensor_reduce(m, y, AX.X, ALU.add))
                    link(nc.vector.tensor_scalar(m, m, 1.0 / LAT, None, ALU.mult))
                    link(nc.vector.tensor_tensor(y, y, m.unsqueeze(2).to_broadcast(wide3), ALU.subtract))
                    link(nc.vector.tensor_tensor(sq[0:HI, :, :], y, y, ALU.mult))
                    link(nc.vector.tensor_reduce(v, sq[0:HI, :, :], AX.X, ALU.add))
                    link(nc.vector.tensor_scalar(v, v, 1.0 / LAT, EPS, ALU.mult, ALU.add))
                    dve.wait_ge(s_mm, 1)
                    link(nc.vector.reciprocal(v, mean[0:HI, :]))
                    link(nc.vector.tensor_tensor(y, y, v.unsqueeze(2).to_broadcast(wide3), ALU.mult))

                @block.scalar
                def _(act):
                    act.wait_ge(s_chain, 7)
                    nc.scalar.activation(mean[0:HI, :], var[0:HI, :], ACT.Sqrt).then_inc(s_mm, 1)

                @block.sync
                def _(sp):
                    sp.wait_ge(s_chain, 9)
                    sp.dma_start(out.rearrange("(h l) f -> h (l f)", l=LO),
                                 pre[0:HI, :, :].rearrange("p l f -> p (l f)")).then_inc(s_rows, 16)
                    sp.wait_ge(s_rows, 16)

        ctx2 = ExitStack()
        with ctx2:
            setup()
        clear_counts()
        general = nc.values_load(flag[0:1, 0:1], min_val=0, max_val=RB * P)

        def first_table():
            with nc.Block() as block:
                @block.sync
                def _(sp):
                    load_table(sp, x)

                @block.vector
                def _(dve):
                    done = [0]

                    def link(ins):
                        done[0] += 1
                        ins.then_inc(s_chain, 1)
                        dve.wait_ge(s_chain, done[0])

                    split_table(dve, link, 16 * n_table)
            clear_counts()

        def other_windows(table):
            with nc.If(general > 0):
                with nc.Fori(1, NW):
                    windows("next")
                    edge_pass(table, False)
                windows("first")

        if NPICK:
            first_table()
        windows("first")
        edge_pass(x, True)
        other_windows(x)
        update(0)
        with nc.Fori(1, DEPTH) as layer:
            edge_pass(nodes_dram, False)
            other_windows(nodes_dram)
            update(layer)
        finish()


_INS = ['x', 'src', 'dst', 'edge_attr_6', 'L0_gnn_kW1', 'L0_gnn_kb1', 'L0_gnn_kW2', 'L0_gnn_kb2',
        'L0_gnn_kW3', 'L0_gnn_kb3', 'L0_gnn_root_W', 'L0_gnn_root_b']


def constant_table(n_nodes, n_edges, lat):
    import numpy as np
    d = layout(n_nodes, n_edges, lat)
    cols, n = constants(n_nodes, n_edges, lat)
    p = np.arange(P)
    table = np.zeros((P, n), np.float32)
    for name, v in (("ident", np.eye(P)),
                    ("slot_tile", p[:, None] // SL == np.arange(TG)[None]),
                    ("slot", (p % SL)[:, None]),
                    ("slots", np.arange(SL)[None]),
                    ("first_of_hi", d["LO"] * np.arange(d["HI"])[None]),
                    ("his", np.arange(d["HI"])[None]),
                    ("los", np.arange(d["LO"])[None]),
                    ("parts", np.arange(PART)[None]),
                    ("chunk_hi", p[:, None] + P * np.arange(d["NC"])[None]),
                    ("own_tile", p[:, None] // lat + TG // 2 * (np.arange(2 * P)[None] // P)
                     == np.arange(2 * P)[None] % P // SL),
                    ("fold", p[:, None] % QUAD == np.arange(lat)[None])):
        table[:, cols[name][0]:cols[name][1]] = v
    return table


def kernel(**inputs):
    import numpy as np
    import concourse.bacc as bacc
    from concourse.bass_utils import run_bass_kernel_spmd

    nc = bacc.Bacc("TRN2", target_bir_lowering=False, num_devices=1)
    n, lat = inputs['x'].shape
    arrays, args = {}, []
    named = [(k, np.ascontiguousarray(inputs[k])) for k in _INS]
    named.append(("constants", constant_table(n, inputs['src'].shape[0], lat)))
    for name, a in named:
        arrays[f"in_{name}_dram"] = a
        args.append(nc.dram_tensor(f"in_{name}_dram", a.shape, mybir.dt.from_np(a.dtype), kind="ExternalInput").ap())
    out = nc.dram_tensor("out_0_dram", (n, lat), F32, kind="ExternalOutput").ap()
    gnn_kernel(nc, *args, out)
    r = run_bass_kernel_spmd(nc, [arrays], core_ids=[0])
    return r.results[0]["out_0_dram"]
```

```python
import concourse.bass as bass
from concourse import mybir
from contextlib import ExitStack

F32 = mybir.dt.float32
BF16 = mybir.dt.bfloat16
F16 = mybir.dt.float16
I32 = mybir.dt.int32
U32 = mybir.dt.uint32
ALU = mybir.AluOpType
ACT = mybir.ActivationFunctionType
AX = mybir.AxisListType

P = 128
TG = 16
SL = 7
PART = 9
NPICK = 7
NPICK_MLP = 3
BANK_PICKS = 3
QUAD = 32
MAGIC = 1.5 * 2 ** 23
NOWHERE = 1.0e6
EPS = 1e-5


def layout(n_nodes, n_edges, lat):
    lo = -(-n_nodes // P)
    hi = n_nodes // lo
    assert hi * lo == n_nodes and (lat + 1) * lo <= 512
    tiles = -(-n_edges // (P * TG)) * TG
    return dict(LO=lo, HI=hi, NT=tiles, NG=tiles // TG, RB=-(-tiles // P),
                NC=-(-n_nodes // (PART * P)))


def constants(n_nodes, n_edges, lat):
    d = layout(n_nodes, n_edges, lat)
    at, cols = 0, {}
    for name, n in (("ident", P), ("slot_tile", TG), ("slot", 1), ("slots", SL),
                    ("his", d["HI"]), ("los", d["LO"]),
                    ("parts", PART), ("chunk_hi", d["NC"]),
                    ("own_tile", TG * SL), ("fold", lat), ("w1_part", 3)):
        cols[name] = (at, at + n)
        at += n
    return cols, at


def at_least(eng, sem, value):
    if not isinstance(value, int) or value > 0:
        eng.wait_ge(sem, value)


def gnn_kernel(nc, x, src, dst, edge_attr, kW1, kb1, kW2, kb2, kW3, kb3, root_W, root_b, consts, out):
    N, LAT = x.shape
    E, ED = edge_attr.shape
    K = kW2.shape[0]
    DEPTH = root_W.shape[0]
    d = layout(N, E, LAT)
    LO, HI, NT, NG, RB = d["LO"], d["HI"], d["NT"], d["NG"], d["RB"]
    cols, ncols = constants(N, E, LAT)
    NW = -(-N // SL)
    FULL, REST = E // P, E % P
    SG = TG * SL
    NL = LO * LAT
    NLD = NL + LO
    PER = TG * LAT
    CB = 8 * LAT
    NCB = -(-NL // CB)
    NC = d["NC"]
    PL = PART * LAT
    PAIRS = (NG - 5) // 2
    assert NG % 2 == 1 and NG >= 7 and K == P and SG <= P

    nodes_dram = nc.dram_tensor("nodes_scratch", (N, LAT), F32).ap()
    part_dram = nc.dram_tensor("src_part_scratch", (NT, P), F16).ap()
    h2_dram = nc.dram_tensor("h2_scratch", (NG * P, TG * K), F32).ap()

    ctx = ExitStack()
    with ctx:
        def sb(name, shape, dt=F32):
            return ctx.enter_context(nc.sbuf_tensor(name, shape, dt))

        def sem(name):
            return ctx.enter_context(nc.semaphore(name))

        cst = sb("cst", [P, ncols])
        ident = cst[:, cols["ident"][0]:cols["ident"][1]]
        slot_tile = cst[:, cols["slot_tile"][0]:cols["slot_tile"][1]]
        slot = cst[:, cols["slot"][0]:cols["slot"][1]]
        slots = cst[:, cols["slots"][0]:cols["slots"][1]]
        his = cst[:, cols["his"][0]:cols["his"][1]]
        los = cst[:, cols["los"][0]:cols["los"][1]]
        parts = cst[:, cols["parts"][0]:cols["parts"][1]]
        chunk_hi = cst[:, cols["chunk_hi"][0]:cols["chunk_hi"][1]]
        own_tile = cst[:, cols["own_tile"][0]:cols["own_tile"][1]]
        w1_part = cst[:, cols["w1_part"][0]:cols["w1_part"][1]]
        fold = cst[:, cols["fold"][0]:cols["fold"][1]]
        ident16 = sb("ident16", [P, P], BF16)
        ones = sb("ones", [P, P])
        w1_left = sb("w1_left", [P, K])
        w1_one = sb("w1_one", [P, K], BF16)
        w1 = sb("w1", [P, K], BF16)
        w2 = sb("w2", [K, K])
        w3 = sb("w3", [K, LAT, QUAD])
        b3 = sb("b3", [P, QUAD])
        b1 = sb("b1", [K, 1])
        b2_rows = sb("b2_rows", [3, K])
        b2_part = sb("b2_part", [3, K], BF16)
        b2_parts = sb("b2_parts", [3, K], BF16)
        ones3 = sb("ones3", [3, P], BF16)
        root = sb("root", [P, DEPTH, P])
        rb = sb("rb", [P, DEPTH, LAT])
        rows_i = sb("rows_i", [P, 2, RB, P], I32)
        rows_f = sb("rows_f", [P, 2, RB, P])
        real = sb("real", [P, RB, P])
        least = sb("least", [P, RB])
        most = sb("most", [P, RB])
        wide = sb("wide", [P, RB])
        wide_any = sb("wide_any", [P, 1])
        narrow = sb("narrow", [P, 1])
        flag = sb("flag", [P, 1], I32)
        diag = sb("diag", [P, RB, P])
        src_e = sb("src_e", [P, NT], U32)
        src_f = sb("src_f", [P, NT])
        src_hi = sb("src_hi", [P, NT])
        src_part = sb("src_part", [P, NT])
        row_hi = sb("row_hi", [P, RB, P])
        row_hi16 = sb("row_hi16", [P, RB, P], F16)
        dst_e = sb("dst_e", [P, NT])
        base0 = sb("base0", [P, NT])
        base = sb("base", [P, NT])
        rel = sb("rel", [P, NT])
        picked = sb("picked", [P, NG, TG])
        node = sb("node", [P, NG])
        node_hi = sb("node_hi", [P, NG])
        node_lo = sb("node_lo", [P, NG])
        attr = [sb(f"attr{b}", [P, TG, ED]) for b in range(2)]
        attr_left = sb("attr_left", [P, 2, TG, ED])
        attr_parts = sb("attr_parts", [P, TG, P // 2], BF16)
        attrT = sb("attrT", [P, TG // 2 * P], BF16)
        h1 = [sb(f"h1_{b}", [K, 4 * P]) for b in range(2)]
        h2 = [sb(f"h2_{b}", [P, TG, K]) for b in range(2)]
        ix = [sb(f"ix{b}", [P, TG], U32) for b in range(2)]
        xe = [sb(f"xe{b}", [P, TG, LAT]) for b in range(2)]
        in_slot = [sb(f"in_slot{b}", [P, TG, SL]) for b in range(2)]
        hi_all = [sb(f"hi_all{b}", [P, NPICK * P], F16) for b in range(2)]
        hot_src = [sb(f"hot_src{b}", [P, NC, NPICK * P], BF16) for b in range(2)]
        hot_part = [sb(f"hot_part{b}", [P, NPICK, PART], BF16) for b in range(2)]
        masked = sb("masked", [P, NPICK, PART, LAT])
        table_f = sb("table_f", [P, NC, PL])
        table_left = sb("table_left", [P, NC, PL])
        table = sb("table", [P, NC, 3, PL], BF16)
        xs = [sb(f"xs{b}", [P, TG, SL, LAT]) for b in range(2)]
        g_sb = [sb(f"g_sb{b}", [K, TG, SL, LAT]) for b in range(2)]
        xsum = sb("xsum", [P, SG])
        slotT = sb("slotT", [P, SG])
        hot_hi = [sb(f"hot_hi{b}", [SG, HI]) for b in range(2)]
        hot_lo = sb("hot_lo", [SG, LO])
        spread = [sb(f"spread{b}", [SG, NLD]) for b in range(2)]
        x0 = sb("x0", [P, LO, LAT])
        xn = sb("xn", [P, LO, LAT])
        agg = sb("agg", [P, NLD])
        inv = sb("inv", [P, LO])
        xT = sb("xT", [P, NCB, HI])
        root_l = sb("root_l", [P, P])
        rb_l = sb("rb_l", [P, LAT])
        pre = sb("pre", [P, LO, LAT])
        mean = sb("mean", [P, LO])
        var = sb("var", [P, LO])
        sq = sb("sq", [P, LO, LAT])

        bank = [ctx.enter_context(nc.psum_tensor(f"bank{i}", [P, 512], F32)) for i in range(8)]
        ps_g = bank[0:2]
        ps_agg = bank[2]
        ps_slot = bank[3][0:SG, 0:LAT]
        ps_deg = bank[3][0:SG, LAT:LAT + 1]
        ps_slotT = bank[3][:, P:P + SG]
        ps_xsum = bank[4][:, 0:SG]
        ps_attrT = bank[4][:, :].bitcast(BF16)
        ps_1, ps_2 = bank[5:7]

        s_chain = sem("s_chain")
        s_const = sem("s_const")
        s_load = sem("s_load")
        s_fill = sem("s_fill")
        s_rows = sem("s_rows")
        s_hi = sem("s_hi")
        s_hi_out = sem("s_hi_out")
        s_mm = sem("s_mm")
        s_copied = sem("s_copied")
        attr_loaded = [sem("attr_loaded0"), sem("attr_loaded1")]
        weights_split = sem("weights_split")
        attr_split = sem("attr_split")
        attr_turned = sem("attr_turned")
        attrT_ready = sem("attrT_ready")
        mm1_done = sem("mm1_done")
        h1_ready = sem("h1_ready")
        mm2_done = sem("mm2_done")
        h2_ready = sem("h2_ready")
        h2_stored = [sem("h2_stored0"), sem("h2_stored1")]
        h2_loaded = [sem("h2_loaded0"), sem("h2_loaded1")]
        ix_ready = sem("ix_ready")
        gathers_begun = sem("gathers_begun")
        gathered = [sem("gathered0"), sem("gathered1")]
        in_slot_ready = sem("in_slot_ready")
        xs_ready = sem("xs_ready")
        table_loaded = sem("table_loaded")
        table_split = sem("table_split")
        hi_loaded = [sem("hi_loaded0"), sem("hi_loaded1")]
        hot_src_ready = sem("hot_src_ready")
        picked_done = sem("picked_done")
        masked_ready = sem("masked_ready")
        selected = sem("selected")
        g_done = sem("g_done")
        g_copied = sem("g_copied")
        xsum_done = sem("xsum_done")
        xsum_masked = sem("xsum_masked")
        slotT_done = sem("slotT_done")
        slotT_copied = sem("slotT_copied")
        slot_done = sem("slot_done")
        hot_ready = sem("hot_ready")
        spread_ready = sem("spread_ready")
        scattered = sem("scattered")
        every = [s_chain, s_const, weights_split, s_load, s_fill, s_rows, s_hi, s_hi_out, s_mm, s_copied, *attr_loaded, attr_split, attr_turned, attrT_ready,
                 mm1_done, h1_ready, mm2_done, h2_ready, *h2_stored, *h2_loaded,
                 ix_ready, gathers_begun, *gathered, in_slot_ready, xs_ready, table_loaded, table_split, *hi_loaded,
                 hot_src_ready, picked_done, masked_ready, selected, g_done, g_copied, xsum_done, xsum_masked,
                 slotT_done, slotT_copied,
                 slot_done, hot_ready, spread_ready, scattered]

        def clear_counts():
            with nc.Block() as block:
                @block.gpsimd
                def _(pool):
                    pool.dma_reset()
                    for s in every:
                        pool.sem_clear(s)

        def divide(link, hi, of, by):
            link(nc.vector.tensor_scalar(hi, of, 1.0 / by, -(by - 1) / 2 / by, ALU.mult, ALU.add))
            link(nc.vector.tensor_scalar(hi, hi, MAGIC, None, ALU.add))
            link(nc.vector.tensor_scalar(hi, hi, -MAGIC, None, ALU.add))

        def window_steps(link, new_base):
            if new_base == "first":
                link(nc.vector.tensor_copy(base[:, :], base0[:, :]))
            if new_base == "next":
                link(nc.vector.tensor_scalar(base[:, :], base[:, :], float(SL), None, ALU.add))
            link(nc.vector.tensor_tensor(rel[:, :], dst_e[:, :], base[:, :], ALU.subtract))
            link(nc.vector.tensor_tensor(picked[:, :, :], base[:, :].rearrange("p (g t) -> p g t", t=TG),
                                         slot_tile.unsqueeze(1).to_broadcast([P, NG, TG]), ALU.mult))
            link(nc.vector.tensor_reduce(node[:, :], picked[:, :, :], AX.X, ALU.add))
            link(nc.vector.tensor_scalar(node[:, :], node[:, :], slot, None, ALU.add))
            divide(link, node_hi[:, :], node[:, :], LO)
            link(nc.vector.scalar_tensor_tensor(node_lo[:, :], node_hi[:, :], -float(LO), node[:, :],
                                                ALU.mult, ALU.add))

        def setup():
            block = ctx2.enter_context(nc.Block())

            @block.sync
            def _(sp):
                sp.wait_ge(s_fill, 2)
                for w, a in enumerate((src, dst)):
                    whole = FULL // P
                    if whole:
                        sp.dma_start(rows_i[:, w, 0:whole, :],
                                     a[0:whole * P * P].rearrange("(g r e) -> r g e", r=P, e=P)).then_inc(s_rows, 16)
                    more = FULL - whole * P
                    if more:
                        sp.dma_start(rows_i[0:more, w, whole, :],
                                     a[whole * P * P:FULL * P].rearrange("(r e) -> r e", e=P)).then_inc(s_rows, 16)
                    if REST:
                        sp.dma_start(rows_i[more:more + 1, w, whole, 0:REST],
                                     a[FULL * P:E].rearrange("(r e) -> r e", r=1)).then_inc(s_rows, 16)
                sp.dma_start(cst[:, :], consts).then_inc(s_const, 16)
                x_rows = x.rearrange("(h l) f -> h (l f)", l=LO)
                sp.dma_start(x0[0:HI, :, :].rearrange("p l f -> p (l f)"), x_rows).then_inc(s_load, 16)
                sp.dma_start(xn[0:HI, :, :].rearrange("p l f -> p (l f)"), x_rows).then_inc(s_load, 16)
                sp.dma_start(rb[:, :, :], root_b.rearrange("(a l) o -> a l o", a=1)
                             .to_broadcast([P, DEPTH, LAT])).then_inc(s_load, 16)
                sp.dma_start(b1[:, :], kb1.rearrange("(k a) -> k a", a=1)).then_inc(s_load, 16)
                sp.dma_start(b2_rows[:, :], kb2.rearrange("(a k) -> a k", a=1).to_broadcast([3, K])).then_inc(s_load, 16)
                sp.wait_ge(s_hi, 1)
                whole, more = NT // P, NT % P
                if whole:
                    sp.dma_start(part_dram[0:whole * P, :].rearrange("(g r) e -> r g e", r=P),
                                 row_hi16[:, 0:whole, :]).then_inc(s_hi_out, 16)
                if more:
                    sp.dma_start(part_dram[whole * P:NT, :], row_hi16[0:more, whole, :]).then_inc(s_hi_out, 16)
                sp.wait_ge(s_hi_out, 16 * (bool(whole) + bool(more)))

            @block.scalar
            def _(act):
                act.dma_start(w2[:, :], kW2).then_inc(s_load, 16)
                act.wait_ge(s_fill, 7)
                act.dma_start(w3[:, :, 0:LAT], kW3.rearrange("k (i o) -> k i o", i=LAT)).then_inc(s_load, 16)
                for h in range(2):
                    for c in range(9):
                        at = P // 2 * h + ED * c
                        act.dma_start(w1_left[at:at + ED, :], kW1).then_inc(s_load, 16)
                for t in range(P // LAT):
                    act.dma_start(b3[LAT * t:LAT * (t + 1), 0:LAT],
                                  kb3.rearrange("(i o) -> i o", i=LAT)).then_inc(s_load, 16)
                for q in range(8):
                    act.dma_start(root[LAT * q:LAT * (q + 1), :, LAT * q:LAT * (q + 1)],
                                  root_W.rearrange("l i o -> i l o")).then_inc(s_load, 16)
                act.wait_ge(s_load, 16 * 41)

            n_rows = 16 * 2 * (bool(FULL // P) + bool(FULL % P) + bool(REST))

            @block.gpsimd
            def _(pool):
                pool.memset(rows_i[:, 0, :, :], 0).then_inc(s_fill, 1)
                pool.memset(rows_i[:, 1, :, :], int(NOWHERE)).then_inc(s_fill, 1)
                pool.memset(ones[:, :], 1.0).then_inc(s_fill, 1)
                pool.memset(w1_left[:, :], 0.0).then_inc(s_fill, 1)
                pool.memset(root[:, :, :], 0.0).then_inc(s_fill, 1)
                pool.memset(w3[:, :, :], 0.0).then_inc(s_fill, 1)
                pool.memset(b3[:, :], 0.0).then_inc(s_fill, 1)
                for b in range(2):
                    pool.memset(attr[b][:, :, :], 0.0)
                pool.memset(ones3[:, :], 1.0)
                pool.memset(attr_parts[:, :, :], 0.0)
                pool.memset(agg[:, :], 0.0)
                pool.memset(table_f[:, :, :], 0.0)

            @block.vector
            def _(dve):
                done = [0]

                def link(ins):
                    done[0] += 1
                    ins.then_inc(s_chain, 1)
                    dve.wait_ge(s_chain, done[0])

                dve.wait_ge(s_rows, n_rows)
                link(nc.vector.tensor_copy(rows_f[:, :, :, :], rows_i[:, :, :, :]))
                link(nc.vector.tensor_reduce(least[:, :], rows_f[:, 1, :, :], AX.X, ALU.min))
                link(nc.vector.scalar_tensor_tensor(real[:, :, :], rows_f[:, 1, :, :], NOWHERE / 2,
                                                    rows_f[:, 1, :, :], ALU.is_lt, ALU.mult))
                link(nc.vector.tensor_reduce(most[:, :], real[:, :, :], AX.X, ALU.max))
                link(nc.vector.tensor_tensor(wide[:, :], most[:, :], least[:, :], ALU.subtract))
                link(nc.vector.tensor_scalar(wide[:, :], wide[:, :], float(SL - 1), None, ALU.is_gt))
                link(nc.vector.tensor_reduce(wide_any[:, :], wide[:, :], AX.X, ALU.add))
                dve.wait_ge(s_const, 16)
                for r in range(RB):
                    link(nc.vector.tensor_scalar(diag[:, r, :], ident, least[:, r:r + 1], None, ALU.mult))
                divide(link, row_hi[:, :, :], rows_f[:, 0, :, :], PART)
                nc.vector.tensor_copy(row_hi16[:, :, :], row_hi[:, :, :]).then_inc(s_hi, 1)
                for r in range(RB):
                    n = min(P, NT - r * P)
                    at = slice(r * P, r * P + n)
                    dve.wait_ge(s_mm, r + 1)
                    nc.vector.tensor_copy(base0[:, at], bank[r % 2][:, 0:n])
                    nc.vector.tensor_copy(src_e[:, at], bank[r % 2][:, P:P + n])
                    nc.vector.tensor_copy(src_f[:, at], bank[r % 2][:, P:P + n])
                    nc.vector.tensor_copy(dst_e[:, at], bank[r % 2][:, 2 * P:2 * P + n]).then_inc(s_copied, 1)
                dve.wait_ge(s_mm, RB + 1)
                link(nc.vector.tensor_copy(flag[:, :], bank[2][:, 0:1]))
                link(nc.vector.tensor_scalar(narrow[:, :], bank[2][:, 0:1], 0.5, None, ALU.is_lt))
                link(nc.vector.tensor_scalar(base0[:, :], base0[:, :], narrow[:, :], None, ALU.mult))
                divide(link, src_hi[:, :], src_f[:, :], PART)
                nc.vector.scalar_tensor_tensor(src_part[:, :], src_hi[:, :], -float(PART), src_f[:, :],
                                               ALU.mult, ALU.add)
                window_steps(link, "first")

            @block.tensor
            def _(pe):
                pe.wait_ge(s_fill, 3)
                pe.wait_ge(s_chain, 7 + RB)
                for r in range(RB):
                    if r >= 2:
                        pe.wait_ge(s_copied, r - 1)
                    nc.tensor.matmul(bank[r % 2][:, 0:P], ones[:, :], diag[:, r, :], start=True, stop=True)
                    nc.tensor.transpose(bank[r % 2][:, P:2 * P], rows_f[:, 0, r, :], ident)
                    nc.tensor.transpose(bank[r % 2][:, 2 * P:3 * P], rows_f[:, 1, r, :], ident).then_inc(s_mm, 1)
                nc.tensor.matmul(bank[2][:, 0:1], ones[:, :], wide_any[:, :], start=True, stop=True).then_inc(s_mm, 1)

        def windows(new_base):
            with nc.Block() as block:
                @block.vector
                def _(dve):
                    done = [0]

                    def link(ins):
                        done[0] += 1
                        ins.then_inc(s_chain, 1)
                        dve.wait_ge(s_chain, done[0])

                    window_steps(link, new_base)
            clear_counts()

        hi_rows, hi_rest = N // PART, N % PART
        n_table = bool(hi_rows // P) + bool(hi_rows % P) + bool(hi_rest)

        def load_table(sp, nodes):
            whole, more = hi_rows // P, hi_rows % P
            if whole:
                sp.dma_start(table_f[:, 0:whole, :], nodes[0:whole * P * PART, :]
                             .rearrange("(c p l) f -> p c (l f)", p=P, l=PART)).then_inc(table_loaded, 16)
            if more:
                sp.dma_start(table_f[0:more, whole, :], nodes[whole * P * PART:hi_rows * PART, :]
                             .rearrange("(p l) f -> p (l f)", l=PART)).then_inc(table_loaded, 16)
            if hi_rest:
                sp.dma_start(table_f[more:more + 1, whole, 0:hi_rest * LAT], nodes[hi_rows * PART:N, :]
                             .rearrange("(p l) f -> p (l f)", p=1)).then_inc(table_loaded, 16)

        def split_table(dve):
            dve.wait_ge(table_loaded, 16 * n_table)
            of = table_f[:, :, :]
            for s in range(3):
                nc.vector.tensor_copy(table[:, :, s, :], of).then_inc(table_split, 1)
                if s < 2:
                    dve.wait_ge(table_split, 2 * s + 1)
                    nc.vector.tensor_tensor(table_left[:, :, :], of, table[:, :, s, :], ALU.subtract)\
                        .then_inc(table_split, 1)
                    dve.wait_ge(table_split, 2 * s + 2)
                    of = table_left[:, :, :]

        def edge_pass(rows, with_mlp, with_degrees):
            sent = NLD if with_degrees else NL
            n_pick = NPICK_MLP if with_mlp else NPICK
            ps_pick = bank[7:8] if with_mlp else bank[5:8]
            n_banks = -(-n_pick // BANK_PICKS)
            bank_tiles = [range(BANK_PICKS * j, min(BANK_PICKS * (j + 1), n_pick)) for j in range(n_banks)]
            n_dma = TG - n_pick
            block_ctx = nc.Block()
            block = block_ctx.__enter__()

            def over_groups(eng, step):
                step(0, 0, 0)
                step(1, 1, 0)
                with eng.Fori(1, 1 + PAIRS) as h:
                    step(h * 2, 0, h)
                    step(h * 2 + 1, 1, h)
                for g in range(NG - 3, NG):
                    step(g, g % 2, g // 2)

            def last_group(g):
                return isinstance(g, int) and g == NG - 1

            @block.sync
            def _(sp):
                def store(g, b):
                    sp.wait_ge(h2_ready, 4 * (g + 1))
                    sp.dma_start(h2_dram[bass.ds(g * P, P), :], h2[b][:, :, :].rearrange("p t k -> p (t k)"))\
                      .then_inc(h2_stored[b], 16)

                def load_hi(g, b):
                    at_least(sp, hot_src_ready, g - 1)
                    sp.dma_start(hi_all[b][:, 0:n_pick * P], part_dram[bass.ds(g * TG + n_dma, n_pick), :]
                                 .rearrange("t e -> (t e)").unsqueeze(0).to_broadcast([P, n_pick * P]))\
                      .then_inc(hi_loaded[b], 16)

                def step(g, b, half):
                    if not last_group(g):
                        load_hi(g + 1, 1 - b)
                    if not with_mlp:
                        at_least(sp, g_done, 4 * (g - 1))
                        sp.dma_start(h2[b][:, :, :].rearrange("p t k -> p (t k)"),
                                     h2_dram[bass.ds(g * P, P), :]).then_inc(h2_loaded[b], 16)
                        return
                    at_least(sp, attr_split, 5 * (g - 1))
                    if last_group(g):
                        t = FULL - g * TG
                        if t:
                            sp.dma_start(attr[b][:, 0:t, 0:ED], edge_attr[g * TG * P:FULL * P, :]
                                         .rearrange("(t e) f -> e t f", e=P)).then_inc(attr_loaded[b], 16)
                        if REST:
                            sp.dma_start(attr[b][0:REST, t, 0:ED], edge_attr[FULL * P:E, :]).then_inc(attr_loaded[b], 16)
                    else:
                        sp.dma_start(attr[b][:, :, 0:ED], edge_attr[bass.ds(g * (TG * P), TG * P), :]
                                     .rearrange("(t e) f -> e t f", e=P)).then_inc(attr_loaded[b], 16)
                    if not isinstance(g, int) or g >= 1:
                        store(g - 1, 1 - b)

                load_hi(0, 0)
                load_table(sp, rows)
                over_groups(sp, step)
                if with_mlp:
                    store(NG - 1, 0)
                    sp.wait_ge(h2_stored[0], 16 * (NG - NG // 2))
                    sp.wait_ge(h2_stored[1], 16 * (NG // 2))

            last_loads = 16 * (bool(FULL - (NG - 1) * TG) + bool(REST))

            @block.gpsimd
            def _(pool):
                def step(g, b, half):
                    at_least(pool, gathered[b], half * (16 * n_dma))
                    nc.gpsimd.tensor_copy(ix[b][:, :], src_e[:, bass.ds(g * TG, TG)]).then_inc(ix_ready, 1)
                    pool.wait_ge(ix_ready, g + 1)
                    at_least(pool, xs_ready, g - 1)
                    at_least(pool, xsum_done, g - 1)
                    pool.sem_inc(gathers_begun, 1)
                    for t in range(n_dma):
                        pool.indirect_dma_start(out=xe[b][:, t, :], out_offset=None, in_=rows,
                                                in_offset=bass.IndirectOffsetOnAxis(ap=ix[b][:, t:t + 1], axis=0))\
                            .then_inc(gathered[b], 16)

                over_groups(pool, step)
                pool.wait_ge(gathered[0], (NG - NG // 2) * 16 * n_dma)
                pool.wait_ge(gathered[1], (NG // 2) * 16 * n_dma)

            @block.scalar
            def _(act):
                def hidden1(g, n):
                    act.wait_ge(mm1_done, g * 4 + (n + 1))
                    at_least(act, mm2_done, g * 4 + (n - 1))
                    nc.scalar.activation(h1[n % 2][:, :], ps_1[:, :], ACT.Gelu_apprx_tanh,
                                         bias=b1[:, :]).then_inc(h1_ready, 1)

                def hidden2(g, n, b, half):
                    if n == 0:
                        at_least(act, g_done, 4 * (g - 1))
                        at_least(act, h2_stored[b], half * 16)
                    act.wait_ge(mm2_done, g * 4 + (n + 1))
                    nc.scalar.activation(h2[b][:, :, :].rearrange("p (m q h) k -> p m h q k", m=2, h=2)[:, n // 2, n % 2, :, :],
                                         ps_2[:, :].rearrange("p (q k) -> p q k", k=K),
                                         ACT.Gelu_apprx_tanh).then_inc(h2_ready, 1)

                def copy_g(g, b, j):
                    act.wait_ge(g_done, g * 4 + (j + 1))
                    nc.scalar.copy(g_sb[b][:, 4 * j:4 * j + 4, :, :].rearrange("k t s i -> k (t s i)"),
                                   ps_g[j % 2][:, 0:4 * SL * LAT]).then_inc(g_copied, 1)

                def step(g, b, half):
                    more = with_mlp and not last_group(g)
                    at_least(act, slotT_done, g - 1)
                    copy_g(g, b, 0)
                    copy_g(g, b, 1)
                    if more:
                        hidden1(g + 1, 0)
                    copy_g(g, b, 2)
                    if more:
                        hidden1(g + 1, 1)
                        hidden2(g + 1, 0, 1 - b, half + b)
                    copy_g(g, b, 3)
                    if more:
                        hidden1(g + 1, 2)
                        hidden2(g + 1, 1, 1 - b, half + b)
                        hidden1(g + 1, 3)
                        hidden2(g + 1, 2, 1 - b, half + b)
                        hidden2(g + 1, 3, 1 - b, half + b)
                    act.wait_ge(slotT_done, g + 1)
                    at_least(act, slot_done, g)
                    nc.scalar.copy(slotT[:, :], ps_slotT).then_inc(slotT_copied, 1)

                if with_mlp:
                    for n in range(5):
                        if n < 4:
                            hidden1(0, n)
                        if n:
                            hidden2(0, n - 1, 0, 0)
                over_groups(act, step)

            @block.vector
            def _(dve):
                def spread_slots(g, b):
                    at_least(dve, scattered, g - 1)
                    nc.vector.tensor_scalar(hot_hi[b][:, :], his[0:SG, :], node_hi[0:SG, bass.ds(g, 1)], None, ALU.is_equal)
                    at_least(dve, spread_ready, g)
                    nc.vector.tensor_scalar(hot_lo[:, :], los[0:SG, :], node_lo[0:SG, bass.ds(g, 1)], None,
                                            ALU.is_equal).then_inc(hot_ready, 1)
                    dve.wait_ge(slot_done, g + 1)
                    dve.wait_ge(hot_ready, g + 1)
                    if with_degrees:
                        nc.vector.tensor_tensor(spread[b][:, NL:NLD], hot_lo[:, :],
                                                ps_deg.to_broadcast([SG, LO]), ALU.mult)
                    nc.vector.tensor_tensor(
                        spread[b][:, 0:NL].rearrange("p (l o) -> p l o", o=LAT),
                        hot_lo[:, :].unsqueeze(2).to_broadcast([SG, LO, LAT]),
                        ps_slot.unsqueeze(1).to_broadcast([SG, LO, LAT]), ALU.mult).then_inc(spread_ready, 1)

                def split_attr(g, b, half):
                    if last_group(g):
                        dve.wait_ge(attr_loaded[b], half * 16 + last_loads)
                    else:
                        dve.wait_ge(attr_loaded[b], half * 16 + 16)
                    at_least(dve, attr_turned, g)
                    of = attr[b][:, :, :]
                    for a in range(3):
                        here = attr_parts[:, :, 3 * ED * a:3 * ED * (a + 1)].rearrange("p t (b f) -> p t b f", f=ED)
                        nc.vector.tensor_copy(here, of.unsqueeze(2).to_broadcast([P, TG, 3, ED]))\
                            .then_inc(attr_split, 1)
                        if a < 2:
                            dve.wait_ge(attr_split, g * 5 + (2 * a + 1))
                            nc.vector.tensor_tensor(attr_left[:, a, :, :], of, here[:, :, 0, :], ALU.subtract)\
                                .then_inc(attr_split, 1)
                            dve.wait_ge(attr_split, g * 5 + (2 * a + 2))
                            of = attr_left[:, a, :, :]

                def split_weights():
                    done = [0]

                    def split(ins):
                        done[0] += 1
                        ins.then_inc(weights_split, 1)
                        dve.wait_ge(weights_split, done[0])

                    split(nc.vector.memset(w1[:, :], 0.0))
                    for s in range(3):
                        split(nc.vector.tensor_copy(w1_one[:, :], w1_left[:, :]))
                        if s < 2:
                            split(nc.vector.tensor_tensor(w1_left[:, :], w1_left[:, :], w1_one[:, :], ALU.subtract))
                        split(nc.vector.scalar_tensor_tensor(w1[:, :], w1_one[:, :], w1_part[:, s:s + 1],
                                                            w1[:, :], ALU.mult, ALU.add))
                    split(nc.vector.tensor_copy(ident16[:, :], ident))
                    split(nc.vector.memset(b2_parts[:, :], 0.0))
                    for s in range(3):
                        split(nc.vector.tensor_copy(b2_part[:, :], b2_rows[:, :]))
                        if s < 2:
                            split(nc.vector.tensor_tensor(b2_rows[:, :], b2_rows[:, :], b2_part[:, :], ALU.subtract))
                        split(nc.vector.scalar_tensor_tensor(b2_parts[:, :], b2_part[:, :], ident[0:3, s:s + 1],
                                                            b2_parts[:, :], ALU.mult, ALU.add))

                def copy_attr(g):
                    dve.wait_ge(attr_turned, g + 1)
                    at_least(dve, mm1_done, g * 4)
                    nc.vector.tensor_copy(attrT[:, :], ps_attrT).then_inc(attrT_ready, 1)

                def hot_sources(g, b, half):
                    at_least(dve, picked_done, (g - 1) * n_banks)
                    at_least(dve, selected, (g - 1) * n_banks)
                    nc.vector.tensor_tensor(
                        hot_part[b][:, 0:n_pick, :],
                        src_part[:, bass.ds(g * TG + n_dma, n_pick)].unsqueeze(2).to_broadcast([P, n_pick, PART]),
                        parts.unsqueeze(1).to_broadcast([P, n_pick, PART]), ALU.is_equal)
                    dve.wait_ge(hi_loaded[b], half * 16 + 16)
                    for c in range(NC):
                        last = nc.vector.tensor_scalar(hot_src[b][:, c, 0:n_pick * P], hi_all[b][:, 0:n_pick * P],
                                                       chunk_hi[:, c:c + 1], None, ALU.is_equal)
                    last.then_inc(hot_src_ready, 1)

                def select(g, b, half):
                    at_least(dve, xsum_done, g - 1)
                    dve.wait_ge(hot_src_ready, g + 1)
                    for j in range(n_banks):
                        n = len(bank_tiles[j])
                        t = slice(BANK_PICKS * j, BANK_PICKS * j + n)
                        dve.wait_ge(picked_done, g * n_banks + (j + 1))
                        at_least(dve, selected, (g - 1) * n_banks + (j + 1))
                        nc.vector.tensor_tensor(
                            masked[:, t, :, :],
                            ps_pick[j][:, 0:n * PL].rearrange("p (t l f) -> p t l f", t=n, l=PART),
                            hot_part[b][:, t, :].unsqueeze(3).to_broadcast([P, n, PART, LAT]), ALU.mult)\
                            .then_inc(masked_ready, 1)
                        dve.wait_ge(masked_ready, g * n_banks + (j + 1))
                        nc.vector.tensor_reduce(xe[b][:, n_dma + BANK_PICKS * j:n_dma + BANK_PICKS * j + n, :],
                                                masked[:, t, :, :].rearrange("p t l f -> p t f l"), AX.X, ALU.add)\
                            .then_inc(selected, 1)

                def slot_products(g, b, half):
                    at_least(dve, slotT_done, g - 1)
                    at_least(dve, g_done, 4 * (g - 1))
                    nc.vector.tensor_tensor(in_slot[b][:, :, :],
                                            rel[:, bass.ds(g * TG, TG)].unsqueeze(2).to_broadcast([P, TG, SL]),
                                            slots.unsqueeze(1).to_broadcast([P, TG, SL]), ALU.is_equal)\
                        .then_inc(in_slot_ready, 1)
                    dve.wait_ge(in_slot_ready, g + 1)
                    dve.wait_ge(gathered[b], half * (16 * n_dma) + 16 * n_dma)
                    dve.wait_ge(selected, (g + 1) * n_banks)
                    for q in range(4):
                        t = slice(4 * q, 4 * q + 4)
                        last = nc.vector.tensor_tensor(
                            xs[b][:, t, :, :],
                            xe[b][:, t, :].unsqueeze(2).to_broadcast([P, 4, SL, LAT]),
                            in_slot[b][:, t, :].unsqueeze(3).to_broadcast([P, 4, SL, LAT]), ALU.mult)
                    last.then_inc(xs_ready, 1)

                def mask_xsum(g):
                    at_least(dve, slotT_done, g)
                    dve.wait_ge(xsum_done, g + 1)
                    nc.vector.tensor_tensor(xsum[:, :], ps_xsum, own_tile, ALU.mult).then_inc(xsum_masked, 1)

                def step(g, b, half):
                    nxt = (g + 1, 1 - b, half + b)
                    more = not last_group(g)
                    mask_xsum(g)
                    if with_mlp and more:
                        copy_attr(g + 1)
                    if not (isinstance(g, int) and g == 0):
                        spread_slots(g - 1, 1 - b)
                    if not isinstance(g, int) or g + 3 < NG:
                        hot_sources(g + 3, 1 - b, half + b + 1)
                    if more:
                        slot_products(*nxt)
                    if with_mlp and (not isinstance(g, int) or g + 2 < NG):
                        split_attr(g + 2, b, half + 1)
                    if not isinstance(g, int) or g + 2 < NG:
                        select(g + 2, b, half + 1)

                if with_mlp:
                    split_weights()
                    split_attr(0, 0, 0)
                    copy_attr(0)
                hot_sources(0, 0, 0)
                split_table(dve)
                hot_sources(1, 1, 0)
                if with_mlp:
                    split_attr(1, 1, 0)
                select(0, 0, 0)
                slot_products(0, 0, 0)
                hot_sources(2, 0, 1)
                select(1, 1, 0)
                over_groups(dve, step)
                spread_slots(NG - 1, 0)
                dve.wait_ge(scattered, NG)
                nc.vector.tensor_tensor(agg[0:HI, 0:sent], agg[0:HI, 0:sent], ps_agg[0:HI, 0:sent], ALU.add)

            @block.tensor
            def _(pe):
                def turn_attr(g):
                    pe.wait_ge(attr_split, 5 * g + 5)
                    at_least(pe, attrT_ready, g)
                    at_least(pe, xsum_masked, g)
                    for r in range(TG // 2):
                        last = nc.tensor.transpose(ps_attrT[:, P * r:P * (r + 1)],
                                                   attr_parts[:, 2 * r:2 * r + 2, :].rearrange("p t f -> p (t f)"),
                                                   ident16[:, :])
                    last.then_inc(attr_turned, 1)

                def product1(g, n):
                    m, h = n // 2, n % 2
                    if n == 0:
                        pe.wait_ge(attrT_ready, g + 1)
                    at_least(pe, h1_ready, g * 4 + n)
                    at = slice(P // 2 * h, P // 2 * h + 9 * ED)
                    nc.tensor.matmul(ps_1[:, :], w1[at, :], attrT[at, 4 * P * m:4 * P * (m + 1)],
                                     start=True, stop=True).then_inc(mm1_done, 1)

                def product2(g, n):
                    pe.wait_ge(h1_ready, g * 4 + (n + 1))
                    at_least(pe, h2_ready, g * 4 + n)
                    nc.tensor.matmul(ps_2[:, :].rearrange("p (q k) -> p q k", k=K), ones3[:, :],
                                     b2_parts[:, :].unsqueeze(1).to_broadcast([3, 4, K]), start=True, stop=False)
                    for q in range(4):
                        last = nc.tensor.matmul(ps_2[:, K * q:K * (q + 1)], h1[n % 2][:, P * q:P * (q + 1)], w2[:, :],
                                                start=False, stop=(q == 3))
                    last.then_inc(mm2_done, 1)

                def scatter(g, b):
                    pe.wait_ge(spread_ready, g + 1)
                    known = isinstance(g, int)
                    nc.tensor.matmul(ps_agg[0:HI, 0:sent], hot_hi[b][:, :], spread[b][:, 0:sent],
                                     start=known and g == 0, stop=known and g == NG - 1).then_inc(scattered, 1)

                def pick(g, b):
                    pe.wait_ge(hot_src_ready, g + 1)
                    for j in range(n_banks):
                        at_least(pe, selected, (g - 1) * n_banks + (j + 1))
                        for t, tile in enumerate(bank_tiles[j]):
                            for c in range(NC):
                                for s in range(3):
                                    last = nc.tensor.matmul(ps_pick[j][:, PL * t:PL * (t + 1)],
                                                            hot_src[b][:, c, P * tile:P * (tile + 1)], table[:, c, s, :],
                                                            start=(c == 0 and s == 0), stop=(c == NC - 1 and s == 2))
                        last.then_inc(picked_done, 1)

                def sum_tiles(g, b, j):
                    at_least(pe, g_copied, g * 4 + (j - 1))
                    for t in range(4):
                        last = nc.tensor.matmul(ps_g[j % 2][:, SL * LAT * t:SL * LAT * (t + 1)], h2[b][:, 4 * j + t, :],
                                                xs[b][:, 4 * j + t, :, :].rearrange("p s i -> p (s i)"),
                                                start=True, stop=True)
                    last.then_inc(g_done, 1)

                def sum_x(g, b, half):
                    at_least(pe, xsum_masked, g)
                    if with_mlp:
                        pe.wait_ge(attrT_ready, g + 1)
                    pe.wait_ge(in_slot_ready, g + 1)
                    pe.wait_ge(gathered[b], half * (16 * n_dma) + 16 * n_dma)
                    pe.wait_ge(selected, (g + 1) * n_banks)
                    for h in range(2):
                        t = slice(TG // 2 * h, TG // 2 * (h + 1))
                        last = nc.tensor.matmul(ps_xsum[:, SG // 2 * h:SG // 2 * (h + 1)],
                                                xe[b][:, t, :].rearrange("p t f -> p (t f)"),
                                                in_slot[b][:, t, :].rearrange("p t s -> p (t s)"),
                                                start=True, stop=True)
                    last.then_inc(xsum_done, 1)

                def slot_messages(g, b):
                    at_least(pe, spread_ready, g)
                    if with_degrees:
                        nc.tensor.matmul(ps_deg, in_slot[b][:, :, :].rearrange("p t s -> p (t s)"), ones[:, 0:1],
                                         start=True, stop=True)
                    pe.wait_ge(g_copied, g * 4 + 4)
                    for i in range(LAT):
                        c = i % 4
                        nc.tensor.matmul(ps_slotT[QUAD * c:QUAD * (c + 1), :], w3[:, i, :],
                                         g_sb[b][:, :, :, i].rearrange("k t s -> k (t s)"),
                                         start=(i < 4), stop=(i >= LAT - 3))
                    pe.wait_ge(xsum_masked, g + 1)
                    nc.tensor.matmul(ps_slotT[0:QUAD, :], b3[:, :], xsum[:, :], start=False, stop=True)\
                      .then_inc(slotT_done, 1)

                def fold_slots(g):
                    pe.wait_ge(slotT_copied, g + 1)
                    nc.tensor.matmul(ps_slot, slotT[:, :], fold, start=True, stop=True).then_inc(slot_done, 1)

                def step(g, b, half):
                    nxt = g + 1
                    more = with_mlp and not last_group(g)
                    if with_mlp:
                        pe.wait_ge(h2_ready, 4 * (g + 1))
                    else:
                        pe.wait_ge(h2_loaded[b], half * 16 + 16)
                    pe.wait_ge(xs_ready, g + 1)
                    sum_tiles(g, b, 0)
                    if not (isinstance(g, int) and g == 0):
                        fold_slots(g - 1)
                    if more:
                        turn_attr(nxt)
                    sum_tiles(g, b, 1)
                    if more:
                        product1(nxt, 0)
                    sum_tiles(g, b, 2)
                    if more:
                        product1(nxt, 1)
                        product2(nxt, 0)
                    sum_tiles(g, b, 3)
                    if more:
                        product1(nxt, 2)
                        product2(nxt, 1)
                    if not isinstance(g, int) or g + 2 < NG:
                        pick(g + 2, b)
                    if more:
                        product1(nxt, 3)
                        product2(nxt, 2)
                    if not (isinstance(g, int) and g == 0):
                        scatter(g - 1, 1 - b)
                    if more:
                        product2(nxt, 3)
                    slot_messages(g, b)
                    if not last_group(g):
                        sum_x(g + 1, 1 - b, half + b)

                if with_mlp:
                    pe.wait_ge(weights_split, 19)
                    turn_attr(0)
                    product1(0, 0)
                pe.wait_ge(table_split, 5)
                pick(0, 0)
                if with_mlp:
                    for n in range(1, 5):
                        if n < 4:
                            product1(0, n)
                        product2(0, n - 1)
                sum_x(0, 0, 0)
                pick(1, 1)
                over_groups(pe, step)
                fold_slots(NG - 1)
                scatter(NG - 1, 0)

            block_ctx.__exit__(None, None, None)

        def update(layer):
            with nc.Block() as block:
                @block.vector
                def _(dve):
                    done = [0]

                    def link(ins):
                        done[0] += 1
                        ins.then_inc(s_chain, 1)
                        dve.wait_ge(s_chain, done[0])

                    nc.vector.tensor_copy(root_l[:, :], root[:, bass.ds(layer, 1), :].rearrange("p a c -> p (a c)"))
                    nc.vector.tensor_copy(rb_l[:, :], rb[:, bass.ds(layer, 1), :].rearrange("p a c -> p (a c)"))\
                        .then_inc(s_copied, 1)
                    for c in range(NCB):
                        n = min(CB, NL - c * CB)
                        dve.wait_ge(s_mm, c + 1)
                        nc.vector.tensor_copy(xT[0:n, c, :], bank[c % 2][0:n, 0:HI]).then_inc(s_copied, 1)
                    if isinstance(layer, int):
                        link(nc.vector.tensor_scalar(inv[0:HI, :], agg[0:HI, NL:NLD], 1.0, None, ALU.max))
                        link(nc.vector.reciprocal(inv[0:HI, :], inv[0:HI, :]))
                    link(nc.vector.tensor_tensor(pre[0:HI, :, :],
                                                 agg[0:HI, 0:NL].rearrange("p (l o) -> p l o", o=LAT),
                                                 inv[0:HI, :].unsqueeze(2).to_broadcast([HI, LO, LAT]), ALU.mult))
                    link(nc.vector.memset(agg[:, :], 0.0))
                    dve.wait_ge(s_mm, 2 * NCB)
                    link(nc.vector.tensor_tensor(pre[0:HI, :, :], pre[0:HI, :, :],
                                                 bank[2][0:HI, 0:NL].rearrange("p (l o) -> p l o", o=LAT), ALU.add))
                    dve.wait_ge(s_copied, 1)
                    link(nc.vector.tensor_tensor(pre[0:HI, :, :], pre[0:HI, :, :],
                                                 rb_l[0:HI, :].unsqueeze(1).to_broadcast([HI, LO, LAT]), ALU.add))

                @block.tensor
                def _(pe):
                    xn_f = xn[:, :, :].rearrange("p l f -> p (l f)")
                    for c in range(NCB):
                        n = min(CB, NL - c * CB)
                        if c >= 2:
                            pe.wait_ge(s_copied, c)
                        nc.tensor.transpose(bank[c % 2][0:n, 0:HI], xn_f[0:HI, c * CB:c * CB + n],
                                            ident[0:HI, 0:HI]).then_inc(s_mm, 1)
                    for c in range(NCB):
                        n = min(CB, NL - c * CB)
                        pe.wait_ge(s_copied, c + 2)
                        nc.tensor.matmul(bank[2][0:HI, c * CB:c * CB + n], xT[0:n, c, :], root_l[0:n, 0:n],
                                         start=True, stop=True).then_inc(s_mm, 1)

                @block.scalar
                def _(act):
                    act.wait_ge(s_chain, 6 if isinstance(layer, int) else 4)
                    nc.scalar.activation(xn[0:HI, :, :], pre[0:HI, :, :], ACT.Gelu_apprx_tanh).then_inc(s_load, 1)

                @block.sync
                def _(sp):
                    sp.wait_ge(s_load, 1)
                    sp.dma_start(nodes_dram.rearrange("(h l) f -> h (l f)", l=LO),
                                 xn[0:HI, :, :].rearrange("p l f -> p (l f)")).then_inc(s_rows, 16)
                    sp.wait_ge(s_rows, 16)
            clear_counts()

        def finish():
            with nc.Block() as block:
                @block.vector
                def _(dve):
                    done = [0]

                    def link(ins):
                        done[0] += 1
                        ins.then_inc(s_chain, 1)
                        dve.wait_ge(s_chain, done[0])

                    y, m, v = pre[0:HI, :, :], mean[0:HI, :], var[0:HI, :]
                    wide3 = [HI, LO, LAT]
                    link(nc.vector.tensor_tensor(y, x0[0:HI, :, :], xn[0:HI, :, :], ALU.add))
                    link(nc.vector.tensor_reduce(m, y, AX.X, ALU.add))
                    link(nc.vector.tensor_scalar(m, m, 1.0 / LAT, None, ALU.mult))
                    link(nc.vector.tensor_tensor(y, y, m.unsqueeze(2).to_broadcast(wide3), ALU.subtract))
                    link(nc.vector.tensor_tensor(sq[0:HI, :, :], y, y, ALU.mult))
                    link(nc.vector.tensor_reduce(v, sq[0:HI, :, :], AX.X, ALU.add))
                    link(nc.vector.tensor_scalar(v, v, 1.0 / LAT, EPS, ALU.mult, ALU.add))
                    dve.wait_ge(s_mm, 1)
                    link(nc.vector.reciprocal(v, mean[0:HI, :]))
                    link(nc.vector.tensor_tensor(y, y, v.unsqueeze(2).to_broadcast(wide3), ALU.mult))

                @block.scalar
                def _(act):
                    act.wait_ge(s_chain, 7)
                    nc.scalar.activation(mean[0:HI, :], var[0:HI, :], ACT.Sqrt).then_inc(s_mm, 1)

                @block.sync
                def _(sp):
                    sp.wait_ge(s_chain, 9)
                    sp.dma_start(out.rearrange("(h l) f -> h (l f)", l=LO),
                                 pre[0:HI, :, :].rearrange("p l f -> p (l f)")).then_inc(s_rows, 16)
                    sp.wait_ge(s_rows, 16)

        ctx2 = ExitStack()
        with ctx2:
            setup()
        clear_counts()
        general = nc.values_load(flag[0:1, 0:1], min_val=0, max_val=RB * P)

        def other_windows(rows, with_degrees):
            with nc.If(general > 0):
                with nc.Fori(1, NW):
                    clear_counts()
                    windows("next")
                    edge_pass(rows, False, with_degrees)
                clear_counts()
                windows("first")

        edge_pass(x, True, True)
        other_windows(x, True)
        update(0)
        with nc.Fori(1, DEPTH) as layer:
            edge_pass(nodes_dram, False, False)
            other_windows(nodes_dram, False)
            update(layer)
        finish()


_INS = ['x', 'src', 'dst', 'edge_attr_6', 'L0_gnn_kW1', 'L0_gnn_kb1', 'L0_gnn_kW2', 'L0_gnn_kb2',
        'L0_gnn_kW3', 'L0_gnn_kb3', 'L0_gnn_root_W', 'L0_gnn_root_b']


def constant_table(n_nodes, n_edges, lat, n_attr):
    import numpy as np
    d = layout(n_nodes, n_edges, lat)
    cols, n = constants(n_nodes, n_edges, lat)
    p = np.arange(P)
    table = np.zeros((P, n), np.float32)
    for name, v in (("ident", np.eye(P)),
                    ("slot_tile", p[:, None] // SL == np.arange(TG)[None]),
                    ("slot", (p % SL)[:, None]),
                    ("slots", np.arange(SL)[None]),
                    ("his", np.arange(d["HI"])[None]),
                    ("los", np.arange(d["LO"])[None]),
                    ("parts", np.arange(PART)[None]),
                    ("chunk_hi", p[:, None] + P * np.arange(d["NC"])[None]),
                    ("own_tile", p[:, None] // lat == np.arange(TG * SL)[None] // SL % (TG // 2)),
                    ("fold", p[:, None] % QUAD == np.arange(lat)[None]),
                    ("w1_part", p[:, None] % (P // 2) // n_attr % 3 == np.arange(3)[None])):
        table[:, cols[name][0]:cols[name][1]] = v
    return table


def kernel(**inputs):
    import numpy as np
    import concourse.bacc as bacc
    from concourse.bass_utils import run_bass_kernel_spmd

    nc = bacc.Bacc("TRN2", target_bir_lowering=False, num_devices=1)
    n, lat = inputs['x'].shape
    arrays, args = {}, []
    named = [(k, np.ascontiguousarray(inputs[k])) for k in _INS]
    named.append(("constants", constant_table(n, inputs['src'].shape[0], lat, inputs['edge_attr_6'].shape[1])))
    for name, a in named:
        arrays[f"in_{name}_dram"] = a
        args.append(nc.dram_tensor(f"in_{name}_dram", a.shape, mybir.dt.from_np(a.dtype), kind="ExternalInput").ap())
    out = nc.dram_tensor("out_0_dram", (n, lat), F32, kind="ExternalOutput").ap()
    gnn_kernel(nc, *args, out)
    r = run_bass_kernel_spmd(nc, [arrays], core_ids=[0])
    return r.results[0]["out_0_dram"]
```
